# Optimizing a Trainium2 kernel written in Bass

```python
import numpy as np
import jax
import jax.numpy as jnp

def _softmax(x, axis=-1):
    return jax.nn.softmax(x, axis=axis)

def _gelu(x):
    return jax.nn.gelu(x, approximate=True)

def _silu(x):
    return jax.nn.silu(x)

def _sigmoid(x):
    return jax.nn.sigmoid(x)

def _layernorm(x, axis=-1, eps=1e-05):
    m = jnp.mean(x, axis=axis, keepdims=True)
    v = jnp.var(x, axis=axis, keepdims=True)
    return (x - m) / jnp.sqrt(v + eps)

def _scatter_add(tgt, idx, src, axis=0):
    return tgt.at[idx].add(src)

def _segment_sum(src, seg, n):
    return jax.ops.segment_sum(src, seg, n)
kernel_name = 'mk_xattn_seq_d2_seqx_r8_e11e2c'

def setup_inputs(seed: int=0):
    np.random.seed(seed)
    _w = jnp.asarray

    def _rec_inputs():
        import jax
        import jax.numpy as jnp
        _rk = jax.random.key(seed)
        x = -0.0002928 + 1 * jax.random.normal(jax.random.fold_in(_rk, 1), (64, 64, 256), jnp.float32)
        _lenS = 64 - jax.random.randint(jax.random.fold_in(_rk, 7), (64,), 0, max(1, 64 // 4) + 1, jnp.int32)
        _lenS2 = 64 - jax.random.randint(jax.random.fold_in(_rk, 8), (64,), 0, max(1, 64 // 4) + 1, jnp.int32)
        _ctx_2048P = jax.random.normal(jax.random.fold_in(_rk, 11), (64, 16, 256), jnp.float32)
        _ctx_2048c = jax.random.dirichlet(jax.random.fold_in(_rk, 511), 0.3 * jnp.ones((16,), jnp.float32), (64, 64))
        _ctx_2048t = jnp.einsum('bsk,bkd->bsd', _ctx_2048c, _ctx_2048P)
        _ctx_2048t = _ctx_2048t * jax.lax.rsqrt(jnp.mean(jnp.square(_ctx_2048t)) + 1e-12) * 0.953939
        ctx_2048 = -1.39393e-06 + 0.999914 * (_ctx_2048t + 0.3 * jax.random.normal(jax.random.fold_in(_rk, 611), (64, 64, 256), jnp.float32))
        _validS = jnp.arange(64)[None, :] < _lenS[:, None]
        _validS2 = jnp.arange(64)[None, :] < _lenS2[:, None]
        _causal = jnp.tril(jnp.ones((64, 64), dtype=bool))
        mask_BxS2_ik0 = jnp.where(jnp.broadcast_to(_validS2[:, :], (64, 64)), 0, 1).astype(jnp.int32)
        return (x, ctx_2048, mask_BxS2_ik0)
    x, ctx_2048, mask_BxS2_ik0 = _rec_inputs()

    def _L0_xattn_setup():
        import jax, jax.numpy as jnp
        import numpy as np
        N, C, S, S2, H, CTX = (4, 64, 256, 256, 8, 64)
        EPS = 1e-05
        key = jax.random.key(seed)
        ks = jax.random.split(key, 6)
        sd = lambda fan: 1.0 / np.sqrt(fan)
        return {'input': jax.random.normal(ks[0], (N, C, S), jnp.float32), 'context': jax.random.normal(ks[1], (N, CTX, S2), jnp.float32), 'gamma': jnp.ones((C,), jnp.float32), 'beta': jnp.zeros((C,), jnp.float32), 'Wq': jax.random.normal(ks[2], (C * H, C), jnp.float32) * sd(C), 'bq': jnp.zeros((C * H,), jnp.float32), 'Wkv': jax.random.normal(ks[3], (C * H * 2, CTX), jnp.float32) * sd(CTX), 'bkv': jnp.zeros((C * H * 2,), jnp.float32), 'Wo': jax.random.normal(ks[4], (C, C * H), jnp.float32) * sd(C * H), 'bo': jnp.zeros((C,), jnp.float32)}
    _L0_xattn_all = _L0_xattn_setup()
    _L0_xattn_in = {k: v for k, v in _L0_xattn_all.items() if k in ('gamma', 'beta', 'Wq', 'bq', 'Wkv', 'bkv', 'Wo', 'bo')}
    del _L0_xattn_all

    def _L1_xattn_setup():
        import jax, jax.numpy as jnp
        import numpy as np
        B, P, K, H, NH = (4, 256, 32, 256, 16)
        DH = H // NH
        EPS = 1e-06

        def rmsnorm(x, w):
            var = jnp.mean(jnp.square(x), axis=-1, keepdims=True)
            return x * jax.lax.rsqrt(var + EPS) * w
        key = jax.random.key(seed)
        ks = jax.random.split(key, 12)
        s = 0.02
        return {'x': jax.random.normal(ks[0], (B, P, H), jnp.float32), 'latents': jax.random.normal(ks[1], (B, K, H), jnp.float32), 'attention_mask': jax.random.randint(ks[2], (B, P), 0, 2, jnp.int32), 'q_w': s * jax.random.normal(ks[3], (H, H), jnp.float32), 'q_b': jnp.zeros((H,), jnp.float32), 'kv_w': s * jax.random.normal(ks[4], (H, 2 * H), jnp.float32), 'kv_b': jnp.zeros((2 * H,), jnp.float32), 'out_w': s * jax.random.normal(ks[5], (H, H), jnp.float32), 'out_b': jnp.zeros((H,), jnp.float32), 'postnorm_w': jnp.ones((H,), jnp.float32), 'mlp_w1': s * jax.random.normal(ks[6], (H, 4 * H), jnp.float32), 'mlp_b1': jnp.zeros((4 * H,), jnp.float32), 'mlp_w2': s * jax.random.normal(ks[7], (4 * H, H), jnp.float32), 'mlp_b2': jnp.zeros((H,), jnp.float32)}
    _L1_xattn_all = _L1_xattn_setup()
    _L1_xattn_in = {k: v for k, v in _L1_xattn_all.items() if k in ('q_w', 'q_b', 'kv_w', 'kv_b', 'out_w', 'out_b', 'postnorm_w', 'mlp_w1', 'mlp_b1', 'mlp_w2', 'mlp_b2')}
    del _L1_xattn_all
    return {'x': x, 'ctx_2048': ctx_2048, 'mask_BxS2_ik0': mask_BxS2_ik0, 'L0_xattn_gamma': _L0_xattn_in['gamma'], 'L0_xattn_beta': _L0_xattn_in['beta'], 'L0_xattn_Wq': _L0_xattn_in['Wq'], 'L0_xattn_bq': _L0_xattn_in['bq'], 'L0_xattn_Wkv': _L0_xattn_in['Wkv'], 'L0_xattn_bkv': _L0_xattn_in['bkv'], 'L0_xattn_Wo': _L0_xattn_in['Wo'], 'L0_xattn_bo': _L0_xattn_in['bo'], 'L1_xattn_q_w': _L1_xattn_in['q_w'], 'L1_xattn_q_b': _L1_xattn_in['q_b'], 'L1_xattn_kv_w': _L1_xattn_in['kv_w'], 'L1_xattn_kv_b': _L1_xattn_in['kv_b'], 'L1_xattn_out_w': _L1_xattn_in['out_w'], 'L1_xattn_out_b': _L1_xattn_in['out_b'], 'L1_xattn_postnorm_w': _L1_xattn_in['postnorm_w'], 'L1_xattn_mlp_w1': _L1_xattn_in['mlp_w1'], 'L1_xattn_mlp_b1': _L1_xattn_in['mlp_b1'], 'L1_xattn_mlp_w2': _L1_xattn_in['mlp_w2'], 'L1_xattn_mlp_b2': _L1_xattn_in['mlp_b2']}

def reference(x, ctx_2048, mask_BxS2_ik0, L0_xattn_gamma, L0_xattn_beta, L0_xattn_Wq, L0_xattn_bq, L0_xattn_Wkv, L0_xattn_bkv, L0_xattn_Wo, L0_xattn_bo, L1_xattn_q_w, L1_xattn_q_b, L1_xattn_kv_w, L1_xattn_kv_b, L1_xattn_out_w, L1_xattn_out_b, L1_xattn_postnorm_w, L1_xattn_mlp_w1, L1_xattn_mlp_b1, L1_xattn_mlp_w2, L1_xattn_mlp_b2):
    import jax
    import jax.numpy as jnp

    def _L0_xattn_ref(input, context, gamma, beta, Wq, bq, Wkv, bkv, Wo, bo):
        import jax, jax.numpy as jnp
        import numpy as np
        N, C, S, S2, H, CTX = (4, 64, 256, 256, 8, 64)
        EPS = 1e-05
        n, c, s = input.shape
        h = H
        mu = jnp.mean(input, axis=(1, 2), keepdims=True)
        var = jnp.var(input, axis=(1, 2), keepdims=True)
        xn = (input - mu) * jax.lax.rsqrt(var + EPS)
        xn = xn * gamma[None, :, None] + beta[None, :, None]
        q = jnp.einsum('oc,ncs->nos', Wq, xn) + bq[None, :, None]
        kv = jnp.einsum('od,nds->nos', Wkv, context) + bkv[None, :, None]
        q = q.reshape(n, h, c, s).transpose(0, 1, 3, 2)
        kv = kv.reshape(n, 2 * h, c, -1).transpose(0, 1, 3, 2)
        k, v = (kv[:, :h], kv[:, h:])
        scale = c ** (-0.25)
        att = jax.nn.softmax(jnp.einsum('nhqc,nhkc->nhqk', q * scale, k * scale), axis=-1)
        y = jnp.einsum('nhqk,nhkc->nhqc', att, v)
        y = y.transpose(0, 1, 3, 2).reshape(n, h * c, s)
        out = jnp.einsum('co,nos->ncs', Wo, y) + bo[None, :, None]
        return input + out

    def _L1_xattn_ref(x, latents, attention_mask, q_w, q_b, kv_w, kv_b, out_w, out_b, postnorm_w, mlp_w1, mlp_b1, mlp_w2, mlp_b2):
        import jax, jax.numpy as jnp
        import numpy as np
        B, P, K, H, NH = (4, 256, 32, 256, 16)
        DH = H // NH
        EPS = 1e-06

        def rmsnorm(x, w):
            var = jnp.mean(jnp.square(x), axis=-1, keepdims=True)
            return x * jax.lax.rsqrt(var + EPS) * w
        b, p, _ = x.shape
        k_len = latents.shape[1]
        residual = latents
        h = jnp.concatenate([x, latents], axis=1)
        q = (latents @ q_w + q_b).reshape(b, k_len, NH, DH)
        kv = (h @ kv_w + kv_b).reshape(b, p + k_len, NH, DH, 2)
        kmat, v = (kv[..., 0], kv[..., 1])
        attn = jnp.einsum('bkhd,bnhd->bhkn', q, kmat) / DH
        full_mask = jnp.concatenate([attention_mask.astype(bool), jnp.ones((b, k_len), bool)], axis=-1)
        attn = jnp.where(full_mask[:, None, None, :], attn, -jnp.inf)
        attn = jax.nn.softmax(attn.astype(jnp.float32), axis=-1).astype(q.dtype)
        attn_out = jnp.einsum('bhkn,bnhd->bkhd', attn, v).reshape(b, k_len, H)
        attn_out = attn_out @ out_w + out_b + residual
        out = rmsnorm(attn_out, postnorm_w)
        out = jax.nn.gelu(out @ mlp_w1 + mlp_b1) @ mlp_w2 + mlp_b2
        return out + residual
    x = _L0_xattn_ref(x, ctx_2048, L0_xattn_gamma, L0_xattn_beta, L0_xattn_Wq, L0_xattn_bq, L0_xattn_Wkv, L0_xattn_bkv, L0_xattn_Wo, L0_xattn_bo)
    x = _L1_xattn_ref(ctx_2048, x, mask_BxS2_ik0, L1_xattn_q_w, L1_xattn_q_b, L1_xattn_kv_w, L1_xattn_kv_b, L1_xattn_out_w, L1_xattn_out_b, L1_xattn_postnorm_w, L1_xattn_mlp_w1, L1_xattn_mlp_b1, L1_xattn_mlp_w2, L1_xattn_mlp_b2)
    return x

_drawn_inputs = setup_inputs


def setup_inputs(seed=0):
    import zlib

    import numpy as np

    out = dict(_drawn_inputs(seed))
    spreads = {'L0_xattn_gamma': (1.0, 0.2),
     'L0_xattn_beta': (0.0, 0.1),
     'L0_xattn_bq': (0.0, 0.1),
     'L0_xattn_bkv': (0.0, 0.1),
     'L0_xattn_bo': (0.0, 0.1),
     'L1_xattn_q_b': (0.0, 0.8),
     'L1_xattn_kv_b': (0.0, 0.8),
     'L1_xattn_out_b': (0.0, 2.0),
     'L1_xattn_postnorm_w': (1.0, 0.6),
     'L1_xattn_mlp_b1': (0.0, 0.1),
     'L1_xattn_mlp_b2': (0.0, 0.1)}
    factors = {'L1_xattn_q_w': 8.0, 'L1_xattn_kv_w': 8.0, 'L1_xattn_out_w': 8.0}
    for name, (base, spread) in spreads.items():
        noise = np.random.default_rng([zlib.crc32(name.encode()), seed]).standard_normal(out[name].shape)
        drawn = base * np.exp(spread * noise) if base else spread * noise
        out[name] = jnp.asarray(drawn.astype(out[name].dtype))
    for name, factor in factors.items():
        out[name] = (out[name] * factor).astype(out[name].dtype)
    return out
```

```python
from contextlib import ExitStack

import concourse.bass as bass
from concourse import mybir

F32 = mybir.dt.float32
F16 = mybir.dt.float16
BF16 = mybir.dt.bfloat16
I32 = mybir.dt.int32
ALU = mybir.AluOpType
ACT = mybir.ActivationFunctionType
AX = mybir.AxisListType

N, C, S = 64, 64, 256
H0 = 8
H1, D1 = 16, 16
FF = 4 * S
G = N // 2
MASKED = -1.0e30
GELU_C, GELU_S = 0.044715, 0.7978845608028654
EPS0, EPS1 = 1e-5, 1e-6

EVEN = ("cT qp0 qp1 SB0 SA0 X1 Q SB1 SA1 K SB2 SA2 V SB3 SA3 U0 SB4 S0 SA4 U1 SB5 S1 SA5 SB6 SA6 S2 U2 "
        "SB7 SA7 S3 U3 SUM mT T0 T1 sT T2 T3 Z0 Z1").split()
ODD = ("cT qp0 qp1 SB0 SA0 PV0 PV1 SB1 SA1 SB2 SA2 SB3 OT SA3 U0 SB4 SA4 U1 OW SB5 SA5 SB6 SA6 U2 AT "
       "SB7 SA7 M1a U3 M1b SUM mT sT Z0 Z1 M2").split()
FRONT = ("cT", "qp0", "qp1", "mT") + tuple(f"SA{h}" for h in range(H0))
BACK = ("SUM", "sT", "Z0", "Z1") + tuple(f"SB{u}" for u in range(8)) + tuple(f"U{p}" for p in range(4))


def slots(par, front=True, back=True, layer1=True):
    for s in (EVEN, ODD)[par]:
        if (front if s in FRONT else back if s in BACK else layer1):
            yield s


LATE = [("e" if par == 0 else "o") + s if s[0] == "Z" else s
        for par in (0, 1) for s in slots(par, front=False) if s[0] == "Z" or s not in BACK]
LATE_FIRST = [s for s in LATE if "Z" in s]
LATE_LAST = [s for s in LATE if "Z" not in s]


def late_use(name, g):
    if isinstance(g, int) and g == 0:
        return LATE_FIRST.index(name)
    order = LATE_LAST if isinstance(g, int) and g == G else LATE
    return len(LATE_FIRST) + len(LATE) * (g - 1) + order.index(name)


def late_bank(name, g):
    if isinstance(g, int) and g == 0:
        return LATE_FIRST.index(name) % 2
    order = LATE_LAST if isinstance(g, int) and g == G else LATE
    return order.index(name) % 2


def build(nc, t):
    ctx = ExitStack()
    with ctx:
        def sb(name, shape, dt=F32):
            return ctx.enter_context(nc.sbuf_tensor(name, shape, dt))

        def sem(name):
            return ctx.enter_context(nc.semaphore(name))

        ctx.enter_context(nc.allow_non_contiguous_dma(reason="bias vectors, one element a partition, once"))

        q_bank = [ctx.enter_context(nc.psum_tensor(f"q_bank{i}", [128, 512], F32)) for i in range(2)]
        s_bank = [ctx.enter_context(nc.psum_tensor(f"s_bank{i}", [128, 512], F32)) for i in range(2)]
        u_bank = ctx.enter_context(nc.psum_tensor("u_bank", [128, 512], F32))
        t_bank = ctx.enter_context(nc.psum_tensor("t_bank", [128, 512], F32))
        l_bank = [ctx.enter_context(nc.psum_tensor(f"l_bank{i}", [128, 512], F32)) for i in range(2)]

        ident = sb("ident", [128, 128])
        stat_ones = sb("stat_ones", [128, 128])
        head_col = sb("head_col", [128, 2, 32])
        head_rows = sb("head_rows", [128, 8])
        ones_row = sb("ones_row", [1, 128], BF16)
        minus_half = sb("minus_half", [128, 1])
        zero_col = sb("zero_col", [128, 1])
        wq = sb("wq", [C, H0, C])
        wk = sb("wk", [C, H0, C])
        wv = sb("wv", [C, H0, C])
        wo = sb("wo", [C, H0 * C])
        woT = sb("woT", [C, H0, C])
        bq = sb("bq", [C, H0])
        bv = sb("bv", [C, H0])
        bo = sb("bo", [1, C])
        gb = sb("gb", [128, 2])
        a_hi_row = sb("a_hi_row", [1, 512], F16)
        w_hi = sb("w_hi", [128, 512], F16)
        w_lo = sb("w_lo", [128, 512], F16)
        bd = sb("bd", [128, 4, 128])
        x_const = sb("x_const", [C + 1, C])
        c0 = sb("c0", [1, C])
        qw = sb("qw", [128, 2, S])
        kvw = sb("kvw", [128, 2, 2 * S])
        kw = sb("kw", [128, 2, S])
        vw = sb("vw", [128, 2, S])
        ow = sb("ow", [128, 2, S])
        w1 = sb("w1", [128, 2, FF])
        w2 = sb("w2", [128, 8, S])
        qb1 = sb("qb1", [128, 2])
        kb1 = sb("kb1", [128, 2])
        b1 = sb("b1", [128, 8])
        kvb = sb("kvb", [128, 2 * S])
        ob = sb("ob", [128, S])
        pw = sb("pw", [128, S])
        b2 = sb("b2", [128, S])
        mask_row = sb("mask_row", [1, G, 2, 2, C], BF16)

        x_all = sb("x_all", [128, G, S])
        bn = sb("bn", [128, G, 2, 3])
        dev = sb("dev", [128, G, 2])
        var_p = sb("var_p", [128, G, 2])
        std = sb("std", [128, G])
        nscale = sb("nscale", [128, G])
        nshift = sb("nshift", [128, G])
        norm = sb("norm", [C, G, 2, 2])

        xr = [sb(f"xr{i}", [C + 1, S]) for i in range(2)]
        c2 = [sb(f"c2{i}", [128, S]) for i in range(2)]
        xn = sb("xn", [C, S])
        xs = sb("xs", [128, S], F16)
        xh = sb("xh", [128, S], F16)
        ch = [sb(f"ch{i}", [128, S], F16) for i in range(2)]
        cl = [sb(f"cl{i}", [128, S], F16) for i in range(2)]
        cx = [sb(f"cx{i}", [128, 2, 2, C]) for i in range(2)]
        qs = [sb(f"qs{i}", [128, H0 * S], F16) for i in range(2)]
        qm = [sb(f"qm{i}", [128, H0 * S], F16) for i in range(2)]
        mx = sb("mx", [128, 2 * H0])
        nm = sb("nm", [2 * H0, 128], F16)
        pT = [x_all[:, i * G // 2:(i + 1) * G // 2, :].rearrange("p (u a) s -> p u (a s)", a=2) for i in range(2)]
        us = sb("us", [128, 4, S])
        ss = sb("ss", [128, S])
        rc = sb("rc", [128, 2, 2, 4])
        zs = sb("zs", [128, 2, H0, C])
        zr = sb("zr", [128, 2, C])

        hT = sb("hT", [128, 2, 4, C])
        x1 = sb("x1", [128, S])
        qT = sb("qT", [128, 2, 128])
        qbd = sb("qbd", [128, 2, 2, 8, C])
        kT = sb("kT", [128, 2, 2, 128])
        vx = sb("vx", [128, 2, 8, 33])
        lmx = sb("lmx", [128, 4, 4])
        sm = [sb(f"sm{i}", [128, 512]) for i in range(2)]
        px = sb("px", [128, 4, 512])
        pt1 = sb("pt1", [128, 4, 512])
        lrc = sb("lrc", [128, 2, 8])
        o1 = sb("o1", [128, S])
        oT = sb("oT", [128, 2, 128])
        ao = sb("ao", [128, S])
        ao_b = sb("ao_b", [128, S])
        sq = sb("sq", [128, S])
        ssq = sb("ssq", [128, 1])
        msq = sb("msq", [128, 1])
        rs = sb("rs", [128, 1])
        an = sb("an", [128, S])
        anT = sb("anT", [128, 2, 128])
        gelu_tiles = sb("gelu_tiles", [128, 4, 2, 512])
        mask_now = sb("mask_now", [1, 2, 128], BF16)
        hu, h2, h3, th = (gelu_tiles[:, i, :, :] for i in range(4))
        mask_i = gelu_tiles[0:1, :, :, :].rearrange("p a b c -> p (a b c)").bitcast(I32).rearrange("p (n c) -> p n c", n=N)
        gg = sb("gg", [128, 8, 128])
        fo = sb("fo", [128, S])
        fo_b = sb("fo_b", [128, S])

        w0_loaded = sem("w0_loaded")
        w1_loaded = sem("w1_loaded")
        xall_loaded = [sem(f"xall_loaded{i}") for i in range(4)]
        const_ready = sem("const_ready")
        memset_done = sem("memset_done")
        prep_pe = sem("prep_pe")
        prep_dve = sem("prep_dve")
        stat_dve = sem("stat_dve")
        bn_done = sem("bn_done")
        stat_pe = sem("stat_pe")
        std_ready = sem("std_ready")
        l1_weights_ready = sem("l1_weights_ready")
        x_loaded = [sem(f"x_loaded{i}") for i in range(2)]
        c_loaded = [sem(f"c_loaded{i}") for i in range(2)]
        xn_ready = sem("xn_ready")
        xpool = sem("xpool")
        cpool = sem("cpool")
        cT_done = sem("cT_done")
        cx_ready = sem("cx_ready")
        q_filled = sem("q_filled")
        qhi_ready = sem("qhi_ready")
        qlo_ready = sem("qlo_ready")
        qm_ready = sem("qm_ready")
        max_done = sem("max_done")
        mT_done = sem("mT_done")
        nm_ready = sem("nm_ready")
        row_loaded = sem("row_loaded")
        s_filled = sem("s_filled")
        exp_done = sem("exp_done")
        u_filled = sem("u_filled")
        us_ready = sem("us_ready")
        rc_ready = sem("rc_ready")
        l_filled = sem("l_filled")
        z_scaled = sem("z_scaled")
        z_summed = sem("z_summed")
        x1T_ready = sem("x1T_ready")
        hc_ready = sem("hc_ready")
        mask_ready = sem("mask_ready")
        x1_ready = sem("x1_ready")
        qT_ready = sem("qT_ready")
        qbd_ready = sem("qbd_ready")
        kT_ready = sem("kT_ready")
        v_ready = sem("v_ready")
        lmax_done = sem("lmax_done")
        lsub_done = sem("lsub_done")
        lexp_done = sem("lexp_done")
        pt_ready = sem("pt_ready")
        lrc_ready = sem("lrc_ready")
        o1_ready = sem("o1_ready")
        oT_ready = sem("oT_ready")
        ao_raw = sem("ao_raw")
        ao_ready = sem("ao_ready")
        ssq_ready = sem("ssq_ready")
        msq_ready = sem("msq_ready")
        rs_ready = sem("rs_ready")
        an_ready = sem("an_ready")
        anT_ready = sem("anT_ready")
        hu_ready = sem("hu_ready")
        h2_ready = sem("h2_ready")
        h3_ready = sem("h3_ready")
        inner_ready = sem("inner_ready")
        th_ready = sem("th_ready")
        gg_ready = sem("gg_ready")
        fo_half = sem("fo_half")
        fo_ready = sem("fo_ready")
        stored = sem("stored")
        waits_met = [sem("waits_met_gpsimd"), sem("waits_met_sync")]

        def at_step(eng, s, per, g, par, j):
            v = 2 * per * g + (per * par + j)
            if not isinstance(g, int) or v > 0:
                eng.wait_ge(s, v)

        def at_pair(eng, s, per, g, j):
            v = per * g + (j - per)
            if not isinstance(g, int) or v > 0:
                eng.wait_ge(s, v)

        def met(eng):
            eng.sem_inc(waits_met[eng is nc.sync], 1)

        drained = {"X1": (x1_ready, 1, 1), "Q": (qT_ready, 2, 2), "K": (kT_ready, 2, 2),
                   "V": (v_ready, 2, 2), "PV0": (o1_ready, 4, 2), "PV1": (o1_ready, 4, 4),
                   "OT": (oT_ready, 1, 1), "OW": (ao_raw, 1, 1), "AT": (anT_ready, 1, 1),
                   "M1a": (hu_ready, 2, 1), "M1b": (hu_ready, 2, 2), "M2": (fo_half, 1, 1),
                   "eZ0": (z_scaled, 4, 1), "eZ1": (z_scaled, 4, 2), "oZ0": (z_scaled, 4, 3),
                   "oZ1": (z_scaled, 4, 4)}
        for i in range(4):
            drained[f"S{i}"] = (lsub_done, 4, i + 1)
            drained[f"T{i}"] = (pt_ready, 4, i + 1)

        def late_free(eng, name, g):
            order = LATE
            if isinstance(g, int) and g in (0, G):
                order = LATE_FIRST if g == 0 else LATE_LAST
            i, back = order.index(name) - 2, 0
            if i < 0:
                back = 1
                before = LATE_FIRST if isinstance(g, int) and g == 1 else LATE
                i += len(before)
                if isinstance(g, int) and g == 0:
                    return l_bank[late_bank(name, g)]
                order = before
            s, per, j = drained[order[i]]
            if "Z" in order[i]:
                v = per * (g - back) + j
            else:
                v = per * (g - back) + (j - per)
            eng.wait_ge(s, v)
            return l_bank[late_bank(name, g)]

        def late_full(eng, name, g):
            eng.wait_ge(l_filled, late_use(name, g) + 1)
            return l_bank[late_bank(name, g)]

        def other(par, g):
            return (g, 1) if par == 0 else (g + 1, 0)

        block = ctx.enter_context(nc.Block())

        def run(loop_on, step, finish=None):
            for g in (0, 1):
                for par in (0, 1):
                    step(g, par, list(slots(par, layer1=g > 0)))
            with loop_on.Fori(2, G - 1) as g:
                for par in (0, 1):
                    step(g, par, list(slots(par)))
            for par in (0, 1):
                step(G - 1, par, list(slots(par, front=par == 0)))
            for par in (0, 1):
                step(G, par, list(slots(par, front=False, back=False)))

        @block.sync
        def _(sp):
            sp.dma_start(wq[:, :, :], t["L0_xattn_Wq"].rearrange("(h o) c -> o h c", h=H0)).then_inc(w0_loaded, 16)
            kv = t["L0_xattn_Wkv"].rearrange("(w h o) d -> w o h d", w=2, h=H0)
            sp.dma_start(wk[:, :, :], kv[0]).then_inc(w0_loaded, 16)
            sp.dma_start(wv[:, :, :], kv[1]).then_inc(w0_loaded, 16)
            sp.dma_start(wo[:, :], t["L0_xattn_Wo"]).then_inc(w0_loaded, 16)
            sp.dma_start(bq[:, :], t["L0_xattn_bq"].rearrange("(h o) -> o h", h=H0)).then_inc(w0_loaded, 16)
            sp.dma_start(bv[:, :], t["L0_xattn_bkv"].rearrange("(w h o) -> w o h", w=2, h=H0)[1]).then_inc(w0_loaded, 16)
            sp.dma_start(bo[:, :], t["L0_xattn_bo"].rearrange("(a c) -> a c", a=1)).then_inc(w0_loaded, 16)
            for r in range(2):
                for j, name in enumerate(("gamma", "beta")):
                    sp.dma_start(gb[r * C:(r + 1) * C, j:j + 1],
                                 t[f"L0_xattn_{name}"].rearrange("(c a) -> c a", a=1)).then_inc(w0_loaded, 16)

            def load_entry(g, par):
                n = 2 * g + par
                sp.dma_start(xr[par][0:C, :], t["x"][bass.ds(n, 1)].rearrange("a c s -> (a c) s")).then_inc(x_loaded[par], 16)
                for r in range(2):
                    sp.dma_start(c2[par][r * C:(r + 1) * C, :],
                                 t["ctx_2048"][bass.ds(n, 1)].rearrange("a c s -> (a c) s")).then_inc(c_loaded[par], 16)

            x_v = t["x"].rearrange("(g r) c s -> (r c) g s", r=2)
            for i in range(4):
                sp.dma_start(x_all[:, 8 * i:8 * i + 8, :], x_v[:, 8 * i:8 * i + 8, :]).then_inc(xall_loaded[i], 16)
                if i == 0:
                    load_entry(0, 0)
                    load_entry(0, 1)
            for dst, name, k in ((qw, "q_w", 2), (kvw, "kv_w", 2), (ow, "out_w", 2), (w1, "mlp_w1", 2), (w2, "mlp_w2", 8)):
                sp.dma_start(dst[:, :, :], t[f"L1_xattn_{name}"].rearrange("(k p) n -> p k n", k=k)).then_inc(w1_loaded, 16)
            sp.dma_start(qb1[:, :], t["L1_xattn_q_b"].rearrange("(k p) -> p k", k=2)).then_inc(w1_loaded, 16)
            sp.dma_start(kb1[:, :], t["L1_xattn_kv_b"].rearrange("(k p w) -> w p k", k=2, w=2)[0]).then_inc(w1_loaded, 16)
            sp.dma_start(b1[:, :], t["L1_xattn_mlp_b1"].rearrange("(k p) -> p k", k=8)).then_inc(w1_loaded, 16)
            for dst, name in ((kvb, "kv_b"), (ob, "out_b"), (pw, "postnorm_w"), (b2, "mlp_b2")):
                sp.dma_start(dst[:, :], t[f"L1_xattn_{name}"].partition_broadcast(128)).then_inc(w1_loaded, 16)
            sp.dma_start(mask_i[:, :, :], t["mask_BxS2_ik0"].rearrange("(a n) s -> a n s", a=1)).then_inc(w1_loaded, 16)

            def row(g, par):
                at_step(sp, nm_ready, 1, g, par, 1)
                met(sp)
                at_step(sp, s_filled, 8, g, par, -8)
                met(sp)
                sp.dma_start(qm[par][C:C + 1, :], nm[:, :]).then_inc(row_loaded, 16)

            sp.wait_ge(memset_done, 6)
            row(0, 0)

            def step(g, par, names):
                last = isinstance(g, int) and g == G - 1
                if not (isinstance(g, int) and g >= G) and not last:
                    at_step(sp, cT_done, 1, g, par, 1)
                    met(sp)
                    at_step(sp, xn_ready, 1, g, par, 1)
                    met(sp)
                    at_step(sp, cpool, 2, g, par, 2)
                    met(sp)
                    load_entry(g + 1, par)
                for s in names:
                    if s == "mT":
                        row(*other(par, g))
                    if s == "M2":
                        at_pair(sp, fo_ready, 1, g, 1)
                        met(sp)
                        dst = t["out"][bass.ds(2 * g - 2, 2)].rearrange("n c s -> (n c) s")
                        sp.dma_start(dst, fo_b[:, :]).then_inc(stored, 16)

            run(sp, step)
            sp.wait_ge(stored, 16 * G)

        @block.gpsimd
        def _(pool):
            pool.memset(ident[:, :], 0.0).then_inc(const_ready, 1)
            pool.memset(head_rows[:, :], 1.0).then_inc(const_ready, 1)
            pool.wait_ge(const_ready, 2)
            pool.affine_select(out=ident[:, :], in_=ident[:, :], compare_op=ALU.not_equal, fill=1.0, base=0,
                               pattern=[[-1, 128]], channel_multiplier=1).then_inc(const_ready, 1)
            pool.affine_select(out=head_rows[:, :], in_=head_rows[:, :], compare_op=ALU.is_ge, fill=0.0, base=0,
                               pattern=[[-D1, 8]], channel_multiplier=1).then_inc(const_ready, 1)
            pool.wait_ge(const_ready, 4)
            pool.affine_select(out=head_rows[:, :], in_=head_rows[:, :], compare_op=ALU.is_ge, fill=0.0, base=D1 - 1,
                               pattern=[[D1, 8]], channel_multiplier=-1).then_inc(const_ready, 1)
            pool.memset(minus_half[:, :], -0.5).then_inc(const_ready, 1)
            pool.memset(vx[:, :, :, 32:33], 1.0).then_inc(const_ready, 1)
            pool.wait_ge(const_ready, 7)
            pool.wait_ge(memset_done, 6)

            def split_entry(g, par):
                at_step(pool, xn_ready, 1, g, par, 1)
                at_step(pool, q_filled, 10, g, par, -8)
                met(pool)
                pool.tensor_scalar(xs[0:C, :], xn[:, :], 1.0, None, ALU.mult).then_inc(xpool, 1)
                pool.tensor_scalar(xh[0:C, :], xn[:, :], 1.0, None, ALU.mult).then_inc(xpool, 1)
                at_step(pool, xpool, 3, g, par, 2)
                met(pool)
                pool.tensor_tensor(xs[C:128, :], xn[:, :], xs[0:C, :], ALU.subtract).then_inc(xpool, 1)
                at_step(pool, xpool, 3, g, par, 3)
                pool.wait_ge(c_loaded[par], 32 * g + 32)
                at_step(pool, s_filled, 8, g, par, -8)
                met(pool)
                pool.tensor_scalar(ch[par][:, :], c2[par][:, :], 1.0, None, ALU.mult).then_inc(cpool, 1)
                at_step(pool, cpool, 2, g, par, 1)
                met(pool)
                pool.tensor_tensor(cl[par][0:C, :], c2[par][0:C, :], ch[par][0:C, :], ALU.subtract).then_inc(cpool, 1)

            def query_copy(g, par, i):
                at_step(pool, qhi_ready, 4, g, par, 2 * i + 2)
                at_step(pool, s_filled, 8, g, par, -8)
                cols = slice(i * 1024, (i + 1) * 1024)
                met(pool)
                pool.tensor_scalar(qm[par][0:C, cols], qs[par][0:C, cols], 1.0, None, ALU.mult).then_inc(qm_ready, 1)

            def step(g, par, names):
                for s in names:
                    if s in ("qp0", "qp1"):
                        query_copy(*other(par, g), int(s[2]))
                    if s == "SUM" and not (isinstance(g, int) and g == G - 1):
                        split_entry(g + 1, par)
                    if s == "SUM":
                        if not (isinstance(g, int) and g == 0):
                            pool.wait_ge(l_filled, late_use("V", g) + 1)
                        at_step(pool, cx_ready, 1, g, par, 1)
                        met(pool)
                        pool.tensor_copy(hT[:, :, 3 * par, :], cx[par][:, 0, :, :]).then_inc(hc_ready, 1)
                    if s == "Q":
                        at_pair(pool, qT_ready, 2, g, 2)
                        pool.wait_ge(l_filled, late_use("oZ1", g - 1) + 1)
                        met(pool)
                        for m in range(2):
                            for h in range(8):
                                pool.tensor_scalar(qbd[:, m, :, h, :],
                                                   qT[:, m, :].rearrange("p (n c) -> p n c", n=2),
                                                   head_rows[:, h:h + 1], None, ALU.mult).then_inc(qbd_ready, 1)
                    if s == "OW":
                        at_pair(pool, ssq_ready, 1, g, 1)
                        at_pair(pool, an_ready, 1, g, 0)
                        met(pool)
                        pool.tensor_scalar(msq[:, :], ssq[:, :], 1.0 / S, EPS1, ALU.mult, ALU.add).then_inc(msq_ready, 1)
                        at_pair(pool, msq_ready, 1, g, 1)
                        met(pool)
                        pool.tensor_tensor(rs[:, :], msq[:, :], minus_half[:, :], ALU.pow).then_inc(rs_ready, 1)
                    if s in ("M1a", "M1b"):
                        i = "ab".index(s[2])
                        at_pair(pool, hu_ready, 2, g, i + 1)
                        at_pair(pool, th_ready, 2, g, i + 1 - 2)
                        met(pool)
                        pool.tensor_tensor(h2[:, i, :], hu[:, i, :], hu[:, i, :], ALU.mult).then_inc(h2_ready, 1)
                        at_pair(pool, h2_ready, 2, g, i + 1)
                        met(pool)
                        pool.tensor_scalar(h3[:, i, :], h2[:, i, :], GELU_C, 1.0, ALU.mult, ALU.add).then_inc(h3_ready, 1)
                        at_pair(pool, h3_ready, 2, g, i + 1)
                        met(pool)
                        pool.tensor_tensor(h2[:, i, :], h3[:, i, :], hu[:, i, :], ALU.mult).then_inc(inner_ready, 1)

            split_entry(0, 0)
            for i in range(2):
                query_copy(0, 0, i)
            split_entry(0, 1)
            run(pool, step)

        @block.scalar
        def _(act):
            act.wait_ge(stat_pe, 2)
            act.wait_ge(memset_done, 6)
            nc.scalar.activation(std[:, :], t_bank[:, 64:64 + G], ACT.Sqrt, bias=zero_col[:, 0:1]).then_inc(std_ready, 1)

            def transposed(g, par):
                at_step(act, cT_done, 1, g, par, 1)
                at_step(act, x1T_ready, 1, g, par, -1)
                at_step(act, hc_ready, 1, g, par, -1)
                at_step(act, u_filled, 4, g, par, -4)
                nc.scalar.activation(cx[par][:, :, :, :].rearrange("p a b c -> p (a b c)"), t_bank[:, 0:256],
                                     ACT.Copy).then_inc(cx_ready, 1)

            def query_high(g, par, i):
                at_step(act, q_filled, 10, g, par, i + 1)
                at_step(act, s_filled, 8, g, par, -8)
                q = qs[par][0:C, i * 1024:(i + 1) * 1024].rearrange("p (a e s) -> p a e s", a=2, e=2)
                for e in range(2):
                    nc.scalar.activation(q[:, :, e, :], q_bank[i][e * C:(e + 1) * C, :].rearrange("p (a s) -> p a s", a=2),
                                         ACT.Copy).then_inc(qhi_ready, 1)

            def neg_max(g, par):
                at_step(act, mT_done, 1, g, par, 1)
                at_step(act, row_loaded, 16, g, par, 0)
                nc.scalar.activation(nm[:, :], t_bank[0:2 * H0, 0:128], ACT.Copy, scale=-1.0).then_inc(nm_ready, 1)

            def step(g, par, names):
                ng, npar = other(par, g)
                for s in names:
                    if s == "cT":
                        transposed(ng, npar)
                    if s in ("qp0", "qp1"):
                        query_high(ng, npar, int(s[2]))
                    if s == "mT":
                        neg_max(ng, npar)
                    if s[:2] == "SB":
                        u = int(s[2])
                        at_step(act, s_filled, 8, g, par, u + 1)
                        at_step(act, u_filled, 4, g, par, -5)
                        nc.scalar.activation(pT[par][:, u, :], s_bank[u % 2][:, :], ACT.Exp,
                                             scale=float(C) ** -0.5).then_inc(exp_done, 1)
                    if s in ("U1", "U3"):
                        i = int(s[1]) // 2
                        at_step(act, u_filled, 4, g, par, i + 1)
                        if not (isinstance(g, int) and g == 0 and par == 0):
                            act.wait_ge(l_filled, late_use("oZ1", g - 1) + 1 if par == 0 else late_use("eZ1", g) + 1)
                        nc.scalar.activation(us[:, 2 * i:2 * i + 2, :].rearrange("p a s -> p (a s)"), u_bank[:, :],
                                             ACT.Copy).then_inc(us_ready, 1)
                    if s == "SUM":
                        at_step(act, u_filled, 4, g, par, 3)
                        at_step(act, u_filled, 4, g, par, 0)
                        nc.scalar.activation(ss[:, :], u_bank[:, 0:S], ACT.Copy).then_inc(us_ready, 1)
                    if s == "Q":
                        b = late_full(act, "Q", g)
                        at_pair(act, qbd_ready, 16, g, 0)
                        for m in range(2):
                            nc.scalar.activation(qT[:, m, :], b[:, m * 128:(m + 1) * 128], ACT.Identity,
                                                 bias=qb1[:, m:m + 1]).then_inc(qT_ready, 1)
                    if s == "K":
                        b = late_full(act, "K", g)
                        for m in range(2):
                            nc.scalar.activation(kT[:, m, :, :].rearrange("p n k -> p (n k)"), b[:, m * 256:(m + 1) * 256],
                                                 ACT.Identity, bias=kb1[:, m:m + 1]).then_inc(kT_ready, 1)
                    if s in ("S0", "S1", "S2", "S3"):
                        i = int(s[1])
                        at_pair(act, lsub_done, 4, g, i + 1)
                        nc.scalar.activation(px[:, i, :], sm[i % 2][:, :], ACT.Exp, scale=1.0 / D1).then_inc(lexp_done, 1)
                    if s in ("T0", "T1", "T2", "T3"):
                        i = int(s[1])
                        b = late_full(act, s, g)
                        nc.scalar.activation(pt1[:, i, :], b[:, :], ACT.Copy).then_inc(pt_ready, 1)
                    if s == "OT":
                        b = late_full(act, "OT", g)
                        nc.scalar.activation(oT[:, :, :].rearrange("p k c -> p (k c)"), b[:, 0:256], ACT.Copy).then_inc(oT_ready, 1)
                    if s == "AT":
                        b = late_full(act, "AT", g)
                        nc.scalar.activation(anT[:, :, :].rearrange("p k c -> p (k c)"), b[:, 0:256], ACT.Copy).then_inc(anT_ready, 1)
                    if s in ("M1b", "M2"):
                        for i in ([0] if s == "M1b" else [1]):
                            at_pair(act, inner_ready, 2, g, i + 1)
                            nc.scalar.activation(th[:, i, :], h2[:, i, :], ACT.Tanh, scale=GELU_S).then_inc(th_ready, 1)

            transposed(0, 0)
            for i in range(2):
                query_high(0, 0, i)
            neg_max(0, 0)
            run(act, step)

        @block.vector
        def _(dve):
            dve.memset(stat_ones[:, :], 0.0).then_inc(stat_dve, 1)
            dve.memset(head_col[:, :, :], 0.0).then_inc(stat_dve, 1)
            dve.memset(mask_row[:, :, :, :, :], 0.0).then_inc(stat_dve, 1)
            dve.memset(bd[:, :, :], 0.0).then_inc(stat_dve, 1)
            for tile in (xh, cl[0], cl[1], qm[0], qm[1], w_lo):
                dve.memset(tile[C:128, :], 0.0).then_inc(stat_dve, 1)
            dve.wait_ge(stat_dve, 10)
            for r in range(2):
                dve.memset(stat_ones[r * C:(r + 1) * C, r * C:(r + 1) * C], 0.5 / C).then_inc(stat_dve, 1)
                dve.memset(head_col[:, r, r:r + 1], 1.0).then_inc(stat_dve, 1)
            dve.memset(ones_row[:, :], 1.0).then_inc(stat_dve, 1)
            dve.memset(xh[C:C + 1, :], 1.0).then_inc(stat_dve, 1)
            dve.memset(xh[96:97, :], 1.0).then_inc(stat_dve, 1)
            for i in range(2):
                dve.memset(xr[i][C:C + 1, :], 1.0).then_inc(memset_done, 1)
                dve.memset(cl[i][C:C + 1, :], 1.0).then_inc(memset_done, 1)
            dve.memset(zero_col[:, :], EPS0).then_inc(memset_done, 1)
            dve.wait_ge(stat_dve, 17)
            dve.memset(zr[:, :, :], 0.0).then_inc(memset_done, 1)

            dve.wait_ge(prep_pe, 1)
            a_t, a_r = q_bank[0], q_bank[1]
            dve.tensor_copy(w_hi[0:C, :], a_t[0:C, :]).then_inc(prep_dve, 1)
            dve.tensor_copy(w_hi[C:128, :], a_t[0:C, :]).then_inc(prep_dve, 1)
            dve.tensor_copy(a_hi_row[:, :], a_r[0:1, :]).then_inc(prep_dve, 1)
            dve.wait_ge(prep_dve, 3)
            dve.tensor_tensor(w_lo[0:C, :], a_t[0:C, :], w_hi[0:C, :], ALU.subtract).then_inc(prep_dve, 1)
            dve.tensor_tensor(w_lo[96:97, :], a_r[0:1, :], a_hi_row[:, :], ALU.subtract).then_inc(prep_dve, 1)
            dve.tensor_copy(w_lo[C:C + 1, :], a_hi_row[:, :]).then_inc(prep_dve, 1)
            dve.wait_ge(prep_pe, 2)
            dve.tensor_copy(woT[:, :, :].rearrange("p h c -> p (h c)"), s_bank[0][0:C, :]).then_inc(prep_dve, 1)
            dve.wait_ge(prep_pe, 4)
            b_t = s_bank[1][0:C, :].rearrange("p (a e c) -> p a e c", a=4, e=2)
            for e in range(2):
                dve.tensor_copy(bd[e * C:(e + 1) * C, :, e * C:(e + 1) * C], b_t[:, :, e, :]).then_inc(prep_dve, 1)
            dve.tensor_tensor(c0[:, :], u_bank[0:1, 0:C], bo[:, :], ALU.add).then_inc(prep_dve, 1)
            dve.wait_ge(const_ready, 7)
            dve.tensor_copy(x_const[0:C, :], ident[0:C, 0:C]).then_inc(prep_dve, 1)
            dve.wait_ge(prep_dve, 11)
            dve.tensor_copy(x_const[C:C + 1, :], c0[:, :]).then_inc(prep_dve, 1)

            for i in range(4):
                dve.wait_ge(xall_loaded[i], 16)
                with dve.Fori(8 * i, 8 * i + 8) as g:
                    dve.bn_stats(bn[:, bass.ds(g, 1), :, :].rearrange("p a b c -> p (a b c)"),
                                 x_all[:, bass.ds(g, 1), :].rearrange("p a s -> p (a s)")).then_inc(bn_done, 1)
            dve.wait_ge(stat_pe, 1)
            dve.wait_ge(bn_done, G)
            dve.tensor_tensor(dev[:, :, :], bn[:, :, :, 1], t_bank[:, 0:G].unsqueeze(2).to_broadcast([128, G, 2]),
                              ALU.subtract).then_inc(stat_dve, 1)
            dve.wait_ge(stat_dve, 18)
            dve.tensor_tensor(var_p[:, :, :], dev[:, :, :], dev[:, :, :], ALU.mult).then_inc(stat_dve, 1)
            dve.wait_ge(stat_dve, 19)
            dve.tensor_scalar(dev[:, :, :], bn[:, :, :, 2], 2.0 / S, None, ALU.mult).then_inc(stat_dve, 1)
            dve.wait_ge(stat_dve, 20)
            dve.tensor_tensor(var_p[:, :, :], var_p[:, :, :], dev[:, :, :], ALU.add).then_inc(stat_dve, 1)
            dve.wait_ge(std_ready, 1)
            dve.reciprocal(nscale[:, :], std[:, :]).then_inc(stat_dve, 1)
            dve.wait_ge(stat_dve, 22)
            dve.wait_ge(w0_loaded, 11 * 16)
            dve.tensor_scalar(nscale[:, :], nscale[:, :], gb[:, 0:1], None, ALU.mult).then_inc(stat_dve, 1)
            dve.wait_ge(stat_dve, 23)
            dve.tensor_tensor(nshift[:, :], t_bank[:, 0:G], nscale[:, :], ALU.mult).then_inc(stat_dve, 1)
            dve.wait_ge(stat_dve, 24)
            dve.tensor_scalar(nshift[:, :], nshift[:, :], -1.0, gb[:, 1:2], ALU.mult, ALU.add).then_inc(stat_dve, 1)
            dve.wait_ge(stat_dve, 25)
            for r in range(2):
                dve.tensor_copy(norm[:, :, r, 0], nscale[r * C:(r + 1) * C, :]).then_inc(stat_dve, 1)
                dve.tensor_copy(norm[:, :, r, 1], nshift[r * C:(r + 1) * C, :]).then_inc(stat_dve, 1)
            dve.wait_ge(stat_dve, 29)

            def normalise(g, par):
                dve.wait_ge(x_loaded[par], 16 * g + 16)
                at_step(dve, xpool, 3, g, par, 0)
                pair = g if isinstance(g, int) else bass.ds(g, 1)
                cols = [norm[:, g:g + 1, par, j] if isinstance(g, int) else norm[:, bass.ds(g, 1), par, j] for j in (0, 1)]
                dve.tensor_scalar(xn[:, :], xr[par][0:C, :], cols[0], cols[1], ALU.mult, ALU.add).then_inc(xn_ready, 1)

            def query_low(g, par, i):
                q = qs[par][:, i * 1024:(i + 1) * 1024].rearrange("p (a e s) -> p a e s", a=2, e=2)
                at_step(dve, qhi_ready, 4, g, par, 2 * i + 2)
                for e in range(2):
                    src = q_bank[i][e * C:(e + 1) * C, :].rearrange("p (a s) -> p a s", a=2)
                    dve.tensor_tensor(q[C:128, :, e, :], src, q[0:C, :, e, :], ALU.subtract).then_inc(qlo_ready, 1)

            def row_max(g, par, h):
                at_step(dve, q_filled, 10, g, par, 3 + h)
                at_step(dve, mT_done, 1, g, par, 0)
                dve.tensor_reduce(mx[:, 2 * h:2 * h + 2], q_bank[h % 2][:, :].rearrange("p (a k) -> p a k", a=2),
                                  AX.X, ALU.max).then_inc(max_done, 1)

            def step(g, par, names):
                ng, npar = other(par, g)
                for s in names:
                    if s in ("qp0", "qp1"):
                        query_low(ng, npar, int(s[2]))
                    if s[:2] == "SA":
                        row_max(ng, npar, int(s[2]))
                    if s == "SB7" and not (isinstance(g, int) and g == G - 1):
                        normalise(g + 1, par)
                    if s == "sT":
                        at_step(dve, u_filled, 4, g, par, 4)
                        at_step(dve, z_scaled, 2, g, par, 0)
                        dve.reciprocal(rc[:, :, :, :],
                                       u_bank[:, 0:256].rearrange("p (q j c) -> p q c j", q=2, j=4)[:, :, 0:2, :]).then_inc(rc_ready, 1)
                    if s in ("Z0", "Z1"):
                        i = int(s[1])
                        b = late_full(dve, "eo"[par] + s, g)
                        at_step(dve, rc_ready, 1, g, par, 1)
                        at_step(dve, z_summed, 2, g, par, 0)
                        dve.tensor_tensor(zs[:, i, :, :], b[:, :].rearrange("p (h c) -> p h c", h=H0),
                                          rc[:, i, :, :].rearrange("p e j -> p (e j)").unsqueeze(2).to_broadcast([128, H0, C]),
                                          ALU.mult).then_inc(z_scaled, 1)
                        at_step(dve, z_scaled, 2, g, par, i + 1)
                        at_step(dve, x1T_ready, 1, g, par, 0)
                        dve.tensor_reduce(zr[:, i, :], zs[:, i, :, :].rearrange("p h c -> p c h"), AX.X, ALU.add).then_inc(z_summed, 1)
                    if s == "Z1":
                        at_step(dve, z_summed, 2, g, par, 2)
                        at_step(dve, cx_ready, 1, g, par, 1)
                        if not (isinstance(g, int) and g == 0):
                            dve.wait_ge(l_filled, late_use("V", g) + 1)
                        dve.tensor_tensor(hT[:, :, 1 + par, :], zr[:, :, :], cx[par][:, 1, :, :], ALU.add).then_inc(x1T_ready, 1)
                    if s == "X1":
                        b = late_full(dve, "X1", g)
                        at_pair(dve, fo_half, 1, g, 0)
                        dve.tensor_copy(x1[:, :], b[:, 0:S]).then_inc(x1_ready, 1)
                        at_pair(dve, pt_ready, 4, g, 0)
                        dve.tensor_scalar(mask_now[:, :, :].rearrange("p n k -> p (n k)"),
                                          mask_row[:, bass.ds(g - 1, 1), :, :, :].rearrange("p g n w c -> p (g n w c)"),
                                          1.0, None, ALU.mult).then_inc(mask_ready, 1)
                    if s == "V":
                        b = late_full(dve, "V", g)
                        bias = kvb[:, :].rearrange("p (h c w) -> p h c w", h=8, w=2)[:, :, :, 1]
                        for n in range(2):
                            dve.tensor_tensor(vx[:, n, :, 0:32], b[:, n * S:(n + 1) * S].rearrange("p (h c) -> p h c", h=8),
                                              bias, ALU.add).then_inc(v_ready, 1)
                    if s in ("S0", "S1", "S2", "S3"):
                        i = int(s[1])
                        b = late_full(dve, s, g)[:, :].rearrange("p (h k) -> p h k", h=4)
                        at_pair(dve, lsub_done, 4, g, i - 3)
                        dve.tensor_reduce(lmx[:, i, :], b, AX.X, ALU.max).then_inc(lmax_done, 1)
                        at_pair(dve, lmax_done, 4, g, i + 1)
                        at_pair(dve, lexp_done, 4, g, i - 1)
                        dve.tensor_tensor(sm[i % 2][:, :].rearrange("p (h k) -> p h k", h=4), b,
                                          lmx[:, i, :].unsqueeze(2).to_broadcast([128, 4, 128]), ALU.subtract).then_inc(lsub_done, 1)
                    if s in ("PV0", "PV1"):
                        n = int(s[2])
                        b = late_full(dve, s, g)[:, 0:264].rearrange("p (h c) -> p h c", h=8)
                        at_pair(dve, o1_ready, 4, g, 2 * n - 2)
                        dve.reciprocal(lrc[:, n, :], b[:, :, 32]).then_inc(lrc_ready, 1)
                        at_pair(dve, lrc_ready, 2, g, n + 1)
                        at_pair(dve, oT_ready, 1, g, 0)
                        for e in range(2):
                            rows = slice(e * C, (e + 1) * C)
                            dve.tensor_tensor(o1[n * C:(n + 1) * C, :].rearrange("p (h e d) -> p h e d", h=8, e=2)[:, :, e, :],
                                              b[rows, :, e * D1:(e + 1) * D1],
                                              lrc[rows, n, :].unsqueeze(2).to_broadcast([C, 8, D1]), ALU.mult).then_inc(o1_ready, 1)
                    if s == "OW":
                        b = late_full(dve, "OW", g)
                        at_pair(dve, an_ready, 1, g, 0)
                        dve.tensor_tensor(ao[:, :], b[:, 0:S], x1[:, :], ALU.add).then_inc(ao_raw, 1)
                        at_pair(dve, ao_raw, 1, g, 1)
                        dve.tensor_tensor(ao_b[:, :], ao[:, :], ob[:, :], ALU.add).then_inc(ao_ready, 1)
                        at_pair(dve, ao_ready, 1, g, 1)
                        at_pair(dve, msq_ready, 1, g, 0)
                        dve.tensor_tensor_reduce(sq[:, :], ao_b[:, :], ao_b[:, :], 1.0, 0.0, ALU.mult, ALU.add,
                                                 ssq[:, :]).then_inc(ssq_ready, 1)
                        at_pair(dve, rs_ready, 1, g, 1)
                        at_pair(dve, anT_ready, 1, g, 0)
                        dve.scalar_tensor_tensor(out=an[:, :], in0=ao_b[:, :], scalar=rs[:, 0:1], in1=pw[:, :],
                                                 op0=ALU.mult, op1=ALU.mult).then_inc(an_ready, 1)
                    if s in ("M1a", "M1b"):
                        i = "ab".index(s[2])
                        b = late_full(dve, s, g)[:, :].rearrange("p (m c) -> p m c", m=4)
                        at_pair(dve, gg_ready, 2, g, i + 1 - 2)
                        dve.tensor_tensor(hu[:, i, :].rearrange("p (m c) -> p m c", m=4), b,
                                          b1[:, 4 * i:4 * i + 4].unsqueeze(2).to_broadcast([128, 4, 128]), ALU.add).then_inc(hu_ready, 1)
                    if s == "M2":
                        for i in range(2):
                            at_pair(dve, th_ready, 2, g, i + 1)
                            at_pair(dve, fo_half, 1, g, 0)
                            dve.scalar_tensor_tensor(out=gg[:, 4 * i:4 * i + 4, :].rearrange("p m c -> p (m c)"), in0=th[:, i, :],
                                                     scalar=1.0, in1=hu[:, i, :], op0=ALU.add, op1=ALU.mult).then_inc(gg_ready, 1)
                        b = late_full(dve, "M2", g)
                        at_pair(dve, fo_ready, 1, g, 0)
                        dve.scalar_tensor_tensor(out=fo[:, :], in0=b[:, 0:S], scalar=0.5, in1=x1[:, :],
                                                 op0=ALU.mult, op1=ALU.add).then_inc(fo_half, 1)
                        at_pair(dve, fo_half, 1, g, 1)
                        at_pair(dve, stored, 16, g, 0)
                        dve.tensor_tensor(fo_b[:, :], fo[:, :], b2[:, :], ALU.add).then_inc(fo_ready, 1)

            normalise(0, 0)
            for i in range(2):
                query_low(0, 0, i)
            normalise(0, 1)
            for h in range(H0):
                row_max(0, 0, h)
            dve.wait_ge(w1_loaded, 13 * 16)
            for k in range(2):
                pair = kvw[:, k, :].rearrange("p (c w) -> p c w", w=2)
                dve.tensor_copy(kw[:, k, :], pair[:, :, 0]).then_inc(l1_weights_ready, 1)
                dve.tensor_copy(vw[:, k, :], pair[:, :, 1]).then_inc(l1_weights_ready, 1)
            for n in range(2):
                dve.tensor_scalar(mask_row[:, :, n, n, :], mask_i.rearrange("p (g r) c -> p g r c", r=2)[:, :, n, :], 0.0, MASKED,
                                  ALU.is_equal, ALU.mult).then_inc(l1_weights_ready, 1)
            run(dve, step)

        @block.tensor
        def _(pe):
            mm = pe.matmul
            pe.wait_ge(w0_loaded, 11 * 16)
            for h in range(H0):
                mm(q_bank[0][0:C, h * C:(h + 1) * C], lhsT=wq[:, h, :], rhs=wk[:, h, :], start=True, stop=True)
                last = mm(q_bank[1][0:1, h * C:(h + 1) * C], lhsT=bq[:, h:h + 1], rhs=wk[:, h, :], start=True, stop=True)
            last.then_inc(prep_pe, 1)
            pe.wait_ge(const_ready, 7)
            for h in range(H0):
                last = pe.transpose(s_bank[0][0:C, h * C:(h + 1) * C], wo[:, h * C:(h + 1) * C], ident[0:C, 0:C])
            last.then_inc(prep_pe, 1)
            pe.wait_ge(prep_dve, 7)
            for h in range(H0):
                last = mm(s_bank[1][0:C, h * C:(h + 1) * C], lhsT=wv[:, h, :], rhs=woT[:, h, :], start=True, stop=True)
            last.then_inc(prep_pe, 1)
            for h in range(H0):
                last = mm(u_bank[0:1, 0:C], lhsT=bv[:, h:h + 1], rhs=woT[:, h, :], start=(h == 0), stop=(h == H0 - 1))
            last.then_inc(prep_pe, 1)
            pe.wait_ge(stat_dve, 17)
            pe.wait_ge(bn_done, G)
            for i in range(2):
                last = mm(t_bank[:, 0:G], lhsT=stat_ones[:, :], rhs=bn[:, :, i, 1], start=(i == 0), stop=(i == 1))
            last.then_inc(stat_pe, 1)
            pe.wait_ge(stat_dve, 21)
            for i in range(2):
                last = mm(t_bank[:, 64:64 + G], lhsT=stat_ones[:, :], rhs=var_p[:, :, i], start=(i == 0), stop=(i == 1))
            last.then_inc(stat_pe, 1)
            pe.wait_ge(prep_dve, 12)
            pe.wait_ge(stat_dve, 29)
            pe.wait_ge(memset_done, 6)

            def transposed(g, par):
                pe.wait_ge(c_loaded[par], 32 * g + 32)
                pe.wait_ge(x_loaded[par], 16 * g + 16)
                at_step(pe, nm_ready, 1, g, par, 0)
                for k in range(2):
                    mm(t_bank[:, 128 + k * C:128 + (k + 1) * C], lhsT=xr[par][:, k * 128:(k + 1) * 128],
                       rhs=x_const[:, :], start=True, stop=True)
                for k in range(2):
                    last = pe.transpose(t_bank[:, k * C:(k + 1) * C], c2[par][0:C, k * 128:(k + 1) * 128], ident[0:C, 0:C])
                last.then_inc(cT_done, 1)

            def queries(g, par, i):
                at_step(pe, xpool, 3, g, par, 3)
                at_step(pe, max_done, 8, g, par, -1 + i)
                for a in range(2):
                    out = q_bank[i][:, a * S:(a + 1) * S]
                    cols = slice((2 * i + a) * 128, (2 * i + a + 1) * 128)
                    mm(out, lhsT=w_hi[:, cols], rhs=xs[:, :], start=True, stop=False)
                    last = mm(out, lhsT=w_lo[:, cols], rhs=xh[:, :], start=False, stop=True)
                last.then_inc(q_filled, 1)

            def scores_by_query(g, par, h):
                at_step(pe, qlo_ready, 4, g, par, 2 if h < 4 else 4)
                if h < 2:
                    at_step(pe, qlo_ready, 4, g, par, 2 * h + 2)
                else:
                    at_step(pe, max_done, 8, g, par, h - 1)
                at_step(pe, cpool, 2, g, par, 1)
                for i in range(2):
                    last = mm(q_bank[h % 2][:, i * S:(i + 1) * S], lhsT=qs[par][:, h * S + i * 128:h * S + (i + 1) * 128],
                              rhs=ch[par][:, :], start=True, stop=True)
                last.then_inc(q_filled, 1)

            def max_rows(g, par):
                at_step(pe, max_done, 8, g, par, 8)
                at_step(pe, cx_ready, 1, g, par, 1)
                pe.transpose(t_bank[0:2 * H0, 0:128], mx[:, :], ident[:, :]).then_inc(mT_done, 1)

            def step(g, par, names):
                ng, npar = other(par, g)
                for s in names:
                    if s == "cT":
                        transposed(ng, npar)
                    if s in ("qp0", "qp1"):
                        queries(ng, npar, int(s[2]))
                    if s[:2] == "SA":
                        scores_by_query(ng, npar, int(s[2]))
                    if s == "mT":
                        max_rows(ng, npar)
                    if s[:2] == "SB":
                        u = int(s[2])
                        p, k = u // 2, u % 2
                        if u == 0:
                            at_step(pe, row_loaded, 16, g, par, 16)
                            at_step(pe, qm_ready, 2, g, par, 2)
                            at_step(pe, cpool, 2, g, par, 2)
                            at_step(pe, qlo_ready, 4, g, par, 4)
                        at_step(pe, exp_done, 8, g, par, u - 1)
                        cols, keys = slice(p * 512, (p + 1) * 512), slice(k * 128, (k + 1) * 128)
                        mm(s_bank[k][:, :], lhsT=ch[par][:, keys], rhs=qs[par][:, cols], start=True, stop=False)
                        mm(s_bank[k][:, :], lhsT=cl[par][:, keys], rhs=qm[par][:, cols], start=False, stop=True).then_inc(s_filled, 1)
                    if s in ("U0", "U1", "U2", "U3"):
                        p = int(s[1])
                        at_step(pe, exp_done, 8, g, par, 2 * p + 2)
                        at_step(pe, cx_ready, 1, g, par, 1)
                        if p == 0:
                            at_step(pe, rc_ready, 1, g, par, 0)
                        if p == 2:
                            at_step(pe, us_ready, 3, g, par, 1)
                        for k in range(2):
                            for e in range(2):
                                last = mm(u_bank[e * C:(e + 1) * C, (p % 2) * S:(p % 2 + 1) * S], lhsT=cx[par][:, 0, k, :],
                                          rhs=pT[par][:, 2 * p + k, e * S:(e + 1) * S], start=(k == 0), stop=(k == 1))
                        if p % 2:
                            last.then_inc(u_filled, 1)
                    if s == "SUM":
                        at_step(pe, us_ready, 3, g, par, 2)
                        for e in range(2):
                            for k in range(2):
                                for j in range(4):
                                    h = 4 * e + j
                                    last = mm(u_bank[32 * j:32 * j + 32, 0:S], lhsT=head_col[:, e, :],
                                              rhs=pT[par][:, 2 * (h // 2) + k, (h % 2) * S:(h % 2 + 1) * S],
                                              start=(e == 0 and k == 0), stop=(e == 1 and k == 1))
                        last.then_inc(u_filled, 1)
                    if s == "sT":
                        at_step(pe, us_ready, 3, g, par, 3)
                        for i in range(2):
                            last = pe.transpose(u_bank[:, i * 128:(i + 1) * 128], ss[:, i * 128:(i + 1) * 128], ident[:, :])
                        last.then_inc(u_filled, 1)
                    if s in ("Z0", "Z1"):
                        i = int(s[1])
                        b = late_free(pe, "eo"[par] + s, g)
                        for p in range(4):
                            last = mm(b[:, p * 128:(p + 1) * 128], lhsT=us[:, p, i * 128:(i + 1) * 128], rhs=bd[:, p, :],
                                      start=True, stop=True)
                        last.then_inc(l_filled, 1)
                    if s == "X1":
                        if isinstance(g, int) and g == 1:
                            pe.wait_ge(l1_weights_ready, 6)
                        at_step(pe, x1T_ready, 1, g, 0, 0)
                        at_step(pe, hc_ready, 1, g, 0, 0)
                        b = late_free(pe, s, g)
                        for k in range(2):
                            last = pe.transpose(b[:, k * 128:(k + 1) * 128], hT[:, k, 1:3, :].rearrange("p n c -> p (n c)"), ident[:, :])
                        last.then_inc(l_filled, 1)
                    if s == "Q":
                        b = late_free(pe, s, g)
                        for m in range(2):
                            for k in range(2):
                                last = mm(b[:, m * 128:(m + 1) * 128], lhsT=qw[:, k, m * 128:(m + 1) * 128],
                                          rhs=hT[:, k, 1:3, :].rearrange("p n c -> p (n c)"), start=(k == 0), stop=(k == 1))
                        last.then_inc(l_filled, 1)
                    if s == "K":
                        b = late_free(pe, s, g)
                        for m in range(2):
                            for k in range(2):
                                last = mm(b[:, m * 256:(m + 1) * 256], lhsT=kw[:, k, m * 128:(m + 1) * 128],
                                          rhs=hT[:, k, :, :].rearrange("p n c -> p (n c)"), start=(k == 0), stop=(k == 1))
                        last.then_inc(l_filled, 1)
                    if s == "V":
                        b = late_free(pe, s, g)
                        for n in range(2):
                            for k in range(2):
                                last = mm(b[:, n * S:(n + 1) * S], lhsT=hT[:, k, 2 * n:2 * n + 2, :].rearrange("p w c -> p (w c)"),
                                          rhs=vw[:, k, :], start=(k == 0), stop=(k == 1))
                        last.then_inc(l_filled, 1)
                    if s in ("S0", "S1", "S2", "S3"):
                        n, m = int(s[1]) // 2, int(s[1]) % 2
                        at_pair(pe, kT_ready, 2, g, 2)
                        at_pair(pe, qbd_ready, 16, g, 8 * m + 8)
                        b = late_free(pe, s, g)
                        at_pair(pe, mask_ready, 1, g, 1)
                        mm(b[:, :].rearrange("p (h k) -> p h k", h=4), lhsT=ones_row[:, :],
                           rhs=mask_now[:, n:n + 1, :].to_broadcast([1, 4, 128]), start=True, stop=True)
                        for i in range(4):
                            last = mm(b[:, i * 128:(i + 1) * 128],
                                      lhsT=qbd[:, m, n, 2 * i:2 * i + 2, :].rearrange("p h c -> p (h c)"),
                                      rhs=kT[:, m, n, :], start=False, stop=True, skip_group_check=True)
                        last.then_inc(l_filled, 1)
                    if s in ("T0", "T1", "T2", "T3"):
                        i = int(s[1])
                        at_pair(pe, lexp_done, 4, g, i + 1)
                        b = late_free(pe, s, g)
                        for j in range(4):
                            last = pe.transpose(b[:, j * 128:(j + 1) * 128], px[:, i, j * 128:(j + 1) * 128], ident[:, :])
                        last.then_inc(l_filled, 1)
                    if s in ("PV0", "PV1"):
                        n = int(s[2])
                        at_pair(pe, pt_ready, 4, g, 2 * n + 2)
                        at_pair(pe, v_ready, 2, g, n + 1)
                        b = late_free(pe, s, g)
                        for i in range(8):
                            last = mm(b[:, i * 33:(i + 1) * 33], lhsT=pt1[:, 2 * n + i // 4, (i % 4) * 128:(i % 4 + 1) * 128],
                                      rhs=vx[:, n, i, :], start=True, stop=True)
                        last.then_inc(l_filled, 1)
                    if s == "OT":
                        at_pair(pe, o1_ready, 4, g, 4)
                        b = late_free(pe, s, g)
                        for k in range(2):
                            last = pe.transpose(b[:, k * 128:(k + 1) * 128], o1[:, k * 128:(k + 1) * 128], ident[:, :])
                        last.then_inc(l_filled, 1)
                    if s == "OW":
                        at_pair(pe, oT_ready, 1, g, 1)
                        b = late_free(pe, s, g)
                        for k in range(2):
                            last = mm(b[:, 0:S], lhsT=oT[:, k, :], rhs=ow[:, k, :], start=(k == 0), stop=(k == 1))
                        last.then_inc(l_filled, 1)
                    if s == "AT":
                        at_pair(pe, an_ready, 1, g, 1)
                        b = late_free(pe, s, g)
                        for k in range(2):
                            last = pe.transpose(b[:, k * 128:(k + 1) * 128], an[:, k * 128:(k + 1) * 128], ident[:, :])
                        last.then_inc(l_filled, 1)
                    if s in ("M1a", "M1b"):
                        i = "ab".index(s[2])
                        at_pair(pe, anT_ready, 1, g, 1)
                        b = late_free(pe, s, g)
                        for j in range(4):
                            m = 4 * i + j
                            for k in range(2):
                                last = mm(b[:, j * 128:(j + 1) * 128], lhsT=w1[:, k, m * 128:(m + 1) * 128], rhs=anT[:, k, :],
                                          start=(k == 0), stop=(k == 1))
                        last.then_inc(l_filled, 1)
                    if s == "M2":
                        b = late_free(pe, s, g)
                        for m in range(8):
                            at_pair(pe, gg_ready, 2, g, m // 4 + 1)
                            last = mm(b[:, 0:S], lhsT=gg[:, m, :], rhs=w2[:, m, :], start=(m == 0), stop=(m == 7))
                        last.then_inc(l_filled, 1)

            transposed(0, 0)
            for i in range(2):
                queries(0, 0, i)
            for h in range(H0):
                scores_by_query(0, 0, h)
            max_rows(0, 0)
            run(pe, step)


INPUTS = ["x", "ctx_2048", "mask_BxS2_ik0", "L0_xattn_gamma", "L0_xattn_beta", "L0_xattn_Wq", "L0_xattn_bq",
          "L0_xattn_Wkv", "L0_xattn_bkv", "L0_xattn_Wo", "L0_xattn_bo", "L1_xattn_q_w", "L1_xattn_q_b",
          "L1_xattn_kv_w", "L1_xattn_kv_b", "L1_xattn_out_w", "L1_xattn_out_b", "L1_xattn_postnorm_w",
          "L1_xattn_mlp_w1", "L1_xattn_mlp_b1", "L1_xattn_mlp_w2", "L1_xattn_mlp_b2"]


def kernel(**inputs):
    import numpy as np
    import concourse.bacc as bacc
    from concourse.bass_utils import run_bass_kernel_spmd

    nc = bacc.Bacc("TRN2", target_bir_lowering=False, num_devices=1)
    arrays, t = {}, {}
    for name in INPUTS:
        a = np.ascontiguousarray(inputs[name])
        arrays[f"in_{name}"] = a
        t[name] = nc.dram_tensor(f"in_{name}", a.shape, mybir.dt.from_np(a.dtype), kind="ExternalInput").ap()
    t["out"] = nc.dram_tensor("out_0", (N, C, S), F32, kind="ExternalOutput").ap()
    build(nc, t)
    r = run_bass_kernel_spmd(nc, [arrays], core_ids=[0])
    return r.results[0]["out_0"]
```

```python
from contextlib import ExitStack

import concourse.bass as bass
from concourse import mybir

F32 = mybir.dt.float32
F16 = mybir.dt.float16
BF16 = mybir.dt.bfloat16
I32 = mybir.dt.int32
ALU = mybir.AluOpType
ACT = mybir.ActivationFunctionType
AX = mybir.AxisListType

N, C, S = 64, 64, 256
H0 = 8
H1, D1 = 16, 16
FF = 4 * S
G = N // 2
MASKED = -1.0e30
GELU_C, GELU_S = 0.044715, 0.7978845608028654
EPS0, EPS1 = 1e-5, 1e-6

ORDER = {
    "pe": (
        "qp0 qp1 X1 cT SB0 Q SB1 SA0 SB2 K SA1 SB3 SB4 U0 V SB5 SA2 SA3 S0 SA4 U1 SA5 SA6 SB6 O0 S1 SB7 S2 U2 "
        "SA7 S3 U3 T0 mT T1 O1 T2 T3 PV0 Z PV1",
        "qp0 cT qp1 SB0 SB1 SB2 OT SA0 SA1 SB3 OW U0 SA2 SB4 SA3 SB5 U1 SB6 AT SA4 SA5 SB7 O0 M1a U2 SA6 SA7 "
        "M1b U3 mT O1 Z M2",
    ),
    "act": (
        "qp0 qp1 cT SB0 SB1 Q HI0 SB2 K SB3 SB4 HI1 SB5 HI2 SB6 S0 SB7 HI3 S1 O0 S2 S3 mT T0 T1 T2 O1 T3",
        "qp0 qp1 SB0 cT SB1 HI0 SB2 OT SB3 HI1 SB4 SB5 HI2 SB6 AT SB7 HI3 O0 mT TH0 O1 TH1",
    ),
    "dve": (
        "qp0 X1 qp1 SA0 LO0 SA1 U0 LO1 V SA2 SA3 SA4 U1 LO2 S0 SA5 S1 SA6 NO LO3 S2 U2 SA7 S3 U3 PV0 PV1 Z",
        "qp0 qp1 SA0 LO0 SA1 OW U0 LO1 RN SA2 SA3 U1 NO LO2 SA4 SA5 M1a LO3 U2 SA6 SA7 U3 M1b GG0 Z GG1 M2",
    ),
    "pool": (
        "Q HC SPL cT",
        "OW M1a cT M1b HC SPL",
    ),
    "sp": (
        "LD qp0 qp1 mT",
        "LD qp0 qp1 mT M2",
    ),
}
FRONT = ("cT", "qp0", "qp1", "mT") + tuple(f"SA{h}" for h in range(H0))
BACK = ("O0", "O1", "Z", "NO", "SPL", "HC", "LD") + tuple(f"SB{u}" for u in range(8)) + tuple(
    f"{x}{p}" for x in ("U", "HI", "LO") for p in range(4))
U_ORDER = ("U0", "U1", "O0", "U2", "U3", "O1")


def slots(eng, par, front=True, back=True, layer1=True):
    for s in ORDER[eng][par].split():
        if (front if s in FRONT else back if s in BACK else layer1):
            yield s


LATE = [("e" if par == 0 else "o") + s if s[0] == "Z" else s
        for par in (0, 1) for s in slots("pe", par, front=False) if s[0] == "Z" or s not in BACK]
LATE_FIRST = [s for s in LATE if "Z" in s]
LATE_LAST = [s for s in LATE if "Z" not in s]


def late_use(name, g):
    if isinstance(g, int) and g == 0:
        return LATE_FIRST.index(name)
    order = LATE_LAST if isinstance(g, int) and g == G else LATE
    return len(LATE_FIRST) + len(LATE) * (g - 1) + order.index(name)


def late_bank(name, g):
    if isinstance(g, int) and g == 0:
        return LATE_FIRST.index(name) % 2
    order = LATE_LAST if isinstance(g, int) and g == G else LATE
    return order.index(name) % 2


def build(nc, t):
    ctx = ExitStack()
    with ctx:
        def sb(name, shape, dt=F32):
            return ctx.enter_context(nc.sbuf_tensor(name, shape, dt))

        def sem(name):
            return ctx.enter_context(nc.semaphore(name))

        ctx.enter_context(nc.allow_non_contiguous_dma(reason="bias vectors, one element a partition, once"))

        q_bank = [ctx.enter_context(nc.psum_tensor(f"q_bank{i}", [128, 512], F32)) for i in range(2)]
        s_bank = [ctx.enter_context(nc.psum_tensor(f"s_bank{i}", [128, 512], F32)) for i in range(2)]
        u_bank = ctx.enter_context(nc.psum_tensor("u_bank", [128, 512], F32))
        t_bank = ctx.enter_context(nc.psum_tensor("t_bank", [128, 512], F32))
        l_bank = [ctx.enter_context(nc.psum_tensor(f"l_bank{i}", [128, 512], F32)) for i in range(2)]

        ident = sb("ident", [128, 128])
        stat_ones = sb("stat_ones", [128, 128])
        head_rows = sb("head_rows", [128, 8])
        ones_row = sb("ones_row", [1, 128], BF16)
        minus_half = sb("minus_half", [128, 1])
        zero_col = sb("zero_col", [128, 1])
        wq = sb("wq", [C, H0, C])
        wk = sb("wk", [C, H0, C])
        wv = sb("wv", [C, H0, C])
        wo = sb("wo", [C, H0 * C])
        woT = sb("woT", [C, H0, C])
        bq = sb("bq", [C, H0])
        bv = sb("bv", [C, H0])
        bo = sb("bo", [1, C])
        gb = sb("gb", [128, 2])
        a_hi_row = sb("a_hi_row", [1, 512], F16)
        w_hi = sb("w_hi", [128, 512], F16)
        w_lo = sb("w_lo", [128, 512], F16)
        bd = sb("bd", [128, 4, C])
        x_const = sb("x_const", [C + 1, C])
        c0 = sb("c0", [1, C])
        qw = sb("qw", [128, 2, S])
        kvw = sb("kvw", [128, 2, 2 * S])
        kw = sb("kw", [128, 2, S])
        vw = sb("vw", [128, 2, S])
        ow = sb("ow", [128, 2, S])
        w1 = sb("w1", [128, 2, FF])
        w2 = sb("w2", [128, 8, S])
        qb1 = sb("qb1", [128, 2])
        kb1 = sb("kb1", [128, 2])
        b1 = sb("b1", [128, 8])
        kvb = sb("kvb", [128, 2 * S])
        ob = sb("ob", [128, S])
        pw = sb("pw", [128, S])
        b2 = sb("b2", [128, S])
        mask_row = sb("mask_row", [1, G, 2, 2, C], BF16)

        x_all = sb("x_all", [128, G, S])
        bn = sb("bn", [128, G, 2, 3])
        dev = sb("dev", [128, G, 2])
        var_p = sb("var_p", [128, G, 2])
        std = sb("std", [128, G])
        nscale = sb("nscale", [128, G])
        nshift = sb("nshift", [128, G])
        norm = sb("norm", [C, G, 2, 2])

        xr = [sb(f"xr{i}", [C + 1, S]) for i in range(2)]
        c2 = [sb(f"c2{i}", [128, S]) for i in range(2)]
        xn = sb("xn", [C, S])
        xs = sb("xs", [128, S], F16)
        xh = sb("xh", [128, S], F16)
        ch = [sb(f"ch{i}", [128, S], F16) for i in range(2)]
        cl = [sb(f"cl{i}", [128, S], F16) for i in range(2)]
        cx = [sb(f"cx{i}", [128, 2, 2, C]) for i in range(2)]
        qs = [sb(f"qs{i}", [128, H0 * S], F16) for i in range(2)]
        qm = [sb(f"qm{i}", [128, H0 * S], F16) for i in range(2)]
        mx = sb("mx", [128, 2 * H0])
        nm = sb("nm", [2 * H0, 128], F16)
        pT = x_all[:, 0:G // 2, :].rearrange("p (h k a) s -> p h k (a s)", h=4, k=2)
        ph, pl = (x_all[:, i * G // 4:(i + 1) * G // 4, :].rearrange("p a s -> p (a s)").bitcast(F16)
                  .rearrange("p (h k s) -> p h k s", h=4, k=2) for i in (2, 3))
        cf = [sb(f"cf{i}", [128, 2, 2, C + 1], F16) for i in range(2)]
        rc = sb("rc", [128, 4, 2, 2])
        on = sb("on", [128, 2, 4, 2, C])
        us = sb("us", [128, 4, S])

        hT = sb("hT", [128, 2, 4, C])
        x1 = sb("x1", [128, S])
        qT = sb("qT", [128, 2, 128])
        qbd = sb("qbd", [128, 2, 2, 8, C])
        kT = sb("kT", [128, 2, 2, 128])
        vx = sb("vx", [128, 2, 8, 33])
        lmx = sb("lmx", [128, 4, 4])
        sm = [sb(f"sm{i}", [128, 512]) for i in range(2)]
        px = sb("px", [128, 4, 512])
        pt1 = sb("pt1", [128, 4, 512])
        lrc = sb("lrc", [128, 2, 8])
        o1 = sb("o1", [128, S])
        oT = sb("oT", [128, 2, 128])
        ao = sb("ao", [128, S])
        ao_b = sb("ao_b", [128, S])
        sq = sb("sq", [128, S])
        ssq = sb("ssq", [128, 1])
        msq = sb("msq", [128, 1])
        rs = sb("rs", [128, 1])
        an = sb("an", [128, S])
        anT = sb("anT", [128, 2, 128])
        gelu_tiles = sb("gelu_tiles", [128, 4, 2, 512])
        mask_now = sb("mask_now", [1, 2, 128], BF16)
        hu, h2, h3, th = (gelu_tiles[:, i, :, :] for i in range(4))
        mask_i = gelu_tiles[0:1, :, :, :].rearrange("p a b c -> p (a b c)").bitcast(I32)[:, 0:N * C].rearrange("p (n c) -> p n c", n=N)
        gg = sb("gg", [128, 8, 128])
        fo = sb("fo", [128, S])
        fo_b = sb("fo_b", [128, S])

        w0_loaded = sem("w0_loaded")
        w1_loaded = sem("w1_loaded")
        xall_loaded = [sem(f"xall_loaded{i}") for i in range(4)]
        const_ready = sem("const_ready")
        memset_done = sem("memset_done")
        prep_pe = sem("prep_pe")
        prep_dve = sem("prep_dve")
        stat_dve = sem("stat_dve")
        bn_done = sem("bn_done")
        stat_pe = sem("stat_pe")
        std_ready = sem("std_ready")
        l1_weights_ready = sem("l1_weights_ready")
        x_loaded = [sem(f"x_loaded{i}") for i in range(2)]
        c_loaded = [sem(f"c_loaded{i}") for i in range(2)]
        xn_ready = sem("xn_ready")
        xpool = sem("xpool")
        cpool = sem("cpool")
        cT_done = sem("cT_done")
        cx_ready = sem("cx_ready")
        q_filled = sem("q_filled")
        qhi_ready = sem("qhi_ready")
        qlo_ready = sem("qlo_ready")
        qm_loaded = [sem(f"qm_loaded{i}") for i in range(2)]
        max_done = sem("max_done")
        mT_done = sem("mT_done")
        nm_ready = sem("nm_ready")
        row_loaded = sem("row_loaded")
        s_filled = sem("s_filled")
        exp_done = sem("exp_done")
        u_filled = sem("u_filled")
        phi_ready = sem("phi_ready")
        plo_ready = sem("plo_ready")
        cf_ready = sem("cf_ready")
        rc_ready = sem("rc_ready")
        on_ready = sem("on_ready")
        us_ready = sem("us_ready")
        l_filled = sem("l_filled")
        x1T_ready = sem("x1T_ready")
        hc_ready = sem("hc_ready")
        mask_ready = sem("mask_ready")
        x1_ready = sem("x1_ready")
        qT_ready = sem("qT_ready")
        qbd_ready = sem("qbd_ready")
        kT_ready = sem("kT_ready")
        v_ready = sem("v_ready")
        lmax_done = sem("lmax_done")
        lsub_done = sem("lsub_done")
        lexp_done = sem("lexp_done")
        pt_ready = sem("pt_ready")
        lrc_ready = sem("lrc_ready")
        o1_ready = sem("o1_ready")
        oT_ready = sem("oT_ready")
        ao_raw = sem("ao_raw")
        ao_ready = sem("ao_ready")
        ssq_ready = sem("ssq_ready")
        msq_ready = sem("msq_ready")
        rs_ready = sem("rs_ready")
        an_ready = sem("an_ready")
        anT_ready = sem("anT_ready")
        hu_ready = sem("hu_ready")
        h2_ready = sem("h2_ready")
        h3_ready = sem("h3_ready")
        inner_ready = sem("inner_ready")
        th_ready = sem("th_ready")
        gg_ready = sem("gg_ready")
        fo_half = sem("fo_half")
        fo_ready = sem("fo_ready")
        stored = sem("stored")
        waits_met = [sem("waits_met_gpsimd"), sem("waits_met_sync")]

        def at_step(eng, s, per, g, par, j):
            v = 2 * per * g + (per * par + j)
            if not isinstance(g, int) or v > 0:
                eng.wait_ge(s, v)

        def at_pair(eng, s, per, g, j):
            v = per * g + (j - per)
            if not isinstance(g, int) or v > 0:
                eng.wait_ge(s, v)

        def met(eng):
            eng.sem_inc(waits_met[eng is nc.sync], 1)

        drained = {"X1": (x1_ready, 1, 1), "Q": (qT_ready, 2, 2), "K": (kT_ready, 2, 2),
                   "V": (v_ready, 2, 2), "PV0": (o1_ready, 4, 2), "PV1": (o1_ready, 4, 4),
                   "OT": (oT_ready, 1, 1), "OW": (ao_raw, 1, 1), "AT": (anT_ready, 1, 1),
                   "M1a": (hu_ready, 2, 1), "M1b": (hu_ready, 2, 2), "M2": (fo_half, 1, 1),
                   "eZ": (x1T_ready, 2, 1), "oZ": (x1T_ready, 2, 2)}
        for i in range(4):
            drained[f"S{i}"] = (lsub_done, 4, i + 1)
            drained[f"T{i}"] = (pt_ready, 4, i + 1)

        def late_free(eng, name, g):
            order = LATE
            if isinstance(g, int) and g in (0, G):
                order = LATE_FIRST if g == 0 else LATE_LAST
            i, back = order.index(name) - 2, 0
            if i < 0:
                back = 1
                before = LATE_FIRST if isinstance(g, int) and g == 1 else LATE
                i += len(before)
                if isinstance(g, int) and g == 0:
                    return l_bank[late_bank(name, g)]
                order = before
            s, per, j = drained[order[i]]
            if "Z" in order[i]:
                v = per * (g - back) + j
            else:
                v = per * (g - back) + (j - per)
            eng.wait_ge(s, v)
            return l_bank[late_bank(name, g)]

        def late_full(eng, name, g):
            eng.wait_ge(l_filled, late_use(name, g) + 1)
            return l_bank[late_bank(name, g)]

        def other(par, g):
            return (g, 1) if par == 0 else (g + 1, 0)

        block = ctx.enter_context(nc.Block())

        def run(eng, name, step):
            for g in (0, 1):
                for par in (0, 1):
                    step(g, par, slots(name, par, layer1=g > 0))
            with eng.Fori(2, G - 1) as g:
                for par in (0, 1):
                    step(g, par, slots(name, par))
            for par in (0, 1):
                step(G - 1, par, slots(name, par, front=par == 0))
            for par in (0, 1):
                step(G, par, slots(name, par, front=False, back=False))

        @block.sync
        def _(sp):
            sp.dma_start(wq[:, :, :], t["L0_xattn_Wq"].rearrange("(h o) c -> o h c", h=H0)).then_inc(w0_loaded, 16)
            kv = t["L0_xattn_Wkv"].rearrange("(w h o) d -> w o h d", w=2, h=H0)
            sp.dma_start(wk[:, :, :], kv[0]).then_inc(w0_loaded, 16)
            sp.dma_start(wv[:, :, :], kv[1]).then_inc(w0_loaded, 16)
            sp.dma_start(wo[:, :], t["L0_xattn_Wo"]).then_inc(w0_loaded, 16)
            sp.dma_start(bq[:, :], t["L0_xattn_bq"].rearrange("(h o) -> o h", h=H0)).then_inc(w0_loaded, 16)
            sp.dma_start(bv[:, :], t["L0_xattn_bkv"].rearrange("(w h o) -> w o h", w=2, h=H0)[1]).then_inc(w0_loaded, 16)
            sp.dma_start(bo[:, :], t["L0_xattn_bo"].rearrange("(a c) -> a c", a=1)).then_inc(w0_loaded, 16)
            for r in range(2):
                for j, name in enumerate(("gamma", "beta")):
                    sp.dma_start(gb[r * C:(r + 1) * C, j:j + 1],
                                 t[f"L0_xattn_{name}"].rearrange("(c a) -> c a", a=1)).then_inc(w0_loaded, 16)

            def load_entry(g, par):
                n = 2 * g + par
                sp.dma_start(xr[par][0:C, :], t["x"][bass.ds(n, 1)].rearrange("a c s -> (a c) s")).then_inc(x_loaded[par], 16)
                for r in range(2):
                    sp.dma_start(c2[par][r * C:(r + 1) * C, :],
                                 t["ctx_2048"][bass.ds(n, 1)].rearrange("a c s -> (a c) s")).then_inc(c_loaded[par], 16)

            x_v = t["x"].rearrange("(g r) c s -> (r c) g s", r=2)
            for i in range(4):
                sp.dma_start(x_all[:, 8 * i:8 * i + 8, :], x_v[:, 8 * i:8 * i + 8, :]).then_inc(xall_loaded[i], 16)
                if i == 0:
                    load_entry(0, 0)
                    load_entry(0, 1)
            for dst, name, k in ((qw, "q_w", 2), (kvw, "kv_w", 2), (ow, "out_w", 2), (w1, "mlp_w1", 2), (w2, "mlp_w2", 8)):
                sp.dma_start(dst[:, :, :], t[f"L1_xattn_{name}"].rearrange("(k p) n -> p k n", k=k)).then_inc(w1_loaded, 16)
            sp.dma_start(qb1[:, :], t["L1_xattn_q_b"].rearrange("(k p) -> p k", k=2)).then_inc(w1_loaded, 16)
            sp.dma_start(kb1[:, :], t["L1_xattn_kv_b"].rearrange("(k p w) -> w p k", k=2, w=2)[0]).then_inc(w1_loaded, 16)
            sp.dma_start(b1[:, :], t["L1_xattn_mlp_b1"].rearrange("(k p) -> p k", k=8)).then_inc(w1_loaded, 16)
            for dst, name in ((kvb, "kv_b"), (ob, "out_b"), (pw, "postnorm_w"), (b2, "mlp_b2")):
                sp.dma_start(dst[:, :], t[f"L1_xattn_{name}"].partition_broadcast(128)).then_inc(w1_loaded, 16)
            sp.dma_start(mask_i[:, :, :], t["mask_BxS2_ik0"].rearrange("(a n) s -> a n s", a=1)).then_inc(w1_loaded, 16)

            def row(g, par):
                at_step(sp, nm_ready, 1, g, par, 1)
                met(sp)
                at_step(sp, s_filled, 8, g, par, -8)
                met(sp)
                sp.dma_start(qm[par][C:C + 1, :], nm[:, :]).then_inc(row_loaded, 16)

            def query_copy(g, par, i):
                at_step(sp, qhi_ready, 4, g, par, 2 * i + 2)
                met(sp)
                at_step(sp, s_filled, 8, g, par, -8)
                met(sp)
                cols = slice(i * 1024, (i + 1) * 1024)
                sp.dma_start(qm[par][0:C, cols], qs[par][0:C, cols]).then_inc(qm_loaded[par], 16)

            for i in range(2):
                query_copy(0, 0, i)
            sp.wait_ge(memset_done, 6)
            row(0, 0)

            def step(g, par, names):
                for s in names:
                    if s == "LD" and not (isinstance(g, int) and g == G - 1):
                        at_step(sp, cT_done, 1, g, par, 1)
                        met(sp)
                        at_step(sp, xn_ready, 1, g, par, 1)
                        met(sp)
                        at_step(sp, cpool, 2, g, par, 2)
                        met(sp)
                        load_entry(g + 1, par)
                    if s in ("qp0", "qp1"):
                        query_copy(*other(par, g), int(s[2]))
                    if s == "mT":
                        row(*other(par, g))
                    if s == "M2":
                        at_pair(sp, fo_ready, 1, g, 1)
                        met(sp)
                        dst = t["out"][bass.ds(2 * g - 2, 2)].rearrange("n c s -> (n c) s")
                        sp.dma_start(dst, fo_b[:, :]).then_inc(stored, 16)

            run(sp, "sp", step)
            sp.wait_ge(stored, 16 * G)

        @block.gpsimd
        def _(pool):
            pool.memset(ident[:, :], 0.0).then_inc(const_ready, 1)
            pool.memset(head_rows[:, :], 1.0).then_inc(const_ready, 1)
            pool.wait_ge(const_ready, 2)
            pool.affine_select(out=ident[:, :], in_=ident[:, :], compare_op=ALU.not_equal, fill=1.0, base=0,
                               pattern=[[-1, 128]], channel_multiplier=1).then_inc(const_ready, 1)
            pool.affine_select(out=head_rows[:, :], in_=head_rows[:, :], compare_op=ALU.is_ge, fill=0.0, base=0,
                               pattern=[[-D1, 8]], channel_multiplier=1).then_inc(const_ready, 1)
            pool.wait_ge(const_ready, 4)
            pool.affine_select(out=head_rows[:, :], in_=head_rows[:, :], compare_op=ALU.is_ge, fill=0.0, base=D1 - 1,
                               pattern=[[D1, 8]], channel_multiplier=-1).then_inc(const_ready, 1)
            pool.memset(minus_half[:, :], -0.5).then_inc(const_ready, 1)
            pool.memset(vx[:, :, :, 32:33], 1.0).then_inc(const_ready, 1)
            pool.wait_ge(const_ready, 7)
            pool.wait_ge(memset_done, 6)

            def split_entry(g, par):
                at_step(pool, xn_ready, 1, g, par, 1)
                at_step(pool, q_filled, 10, g, par, -8)
                met(pool)
                pool.tensor_scalar(xs[0:C, :], xn[:, :], 1.0, None, ALU.mult).then_inc(xpool, 1)
                pool.tensor_scalar(xh[0:C, :], xn[:, :], 1.0, None, ALU.mult).then_inc(xpool, 1)
                at_step(pool, xpool, 3, g, par, 2)
                met(pool)
                pool.tensor_tensor(xs[C:128, :], xn[:, :], xs[0:C, :], ALU.subtract).then_inc(xpool, 1)
                at_step(pool, xpool, 3, g, par, 3)
                pool.wait_ge(c_loaded[par], 32 * g + 32)
                at_step(pool, s_filled, 8, g, par, -8)
                met(pool)
                pool.tensor_scalar(ch[par][:, :], c2[par][:, :], 1.0, None, ALU.mult).then_inc(cpool, 1)
                at_step(pool, cpool, 2, g, par, 1)
                met(pool)
                pool.tensor_tensor(cl[par][0:C, :], c2[par][0:C, :], ch[par][0:C, :], ALU.subtract).then_inc(cpool, 1)

            def context_parts(g, par):
                at_step(pool, cx_ready, 1, g, par, 1)
                at_step(pool, u_filled, 6, g, par, -7)
                met(pool)
                pool.tensor_scalar(cf[par][:, 0, :, 0:C], cx[par][:, 0, :, :], 1.0, None, ALU.mult).then_inc(cf_ready, 1)
                at_step(pool, cf_ready, 2, g, par, 1)
                pool.tensor_tensor(cf[par][:, 1, :, 0:C], cx[par][:, 0, :, :], cf[par][:, 0, :, 0:C],
                                   ALU.subtract).then_inc(cf_ready, 1)

            def step(g, par, names):
                for s in names:
                    if s == "cT":
                        context_parts(*other(par, g))
                    if s == "SPL" and not (isinstance(g, int) and g == G - 1):
                        split_entry(g + 1, par)
                    if s == "HC":
                        if not (isinstance(g, int) and g == 0):
                            pool.wait_ge(l_filled, late_use("V", g) + 1)
                        at_step(pool, cx_ready, 1, g, par, 1)
                        met(pool)
                        pool.tensor_copy(hT[:, :, 3 * par, :], cx[par][:, 0, :, :]).then_inc(hc_ready, 1)
                    if s == "Q":
                        at_pair(pool, qT_ready, 2, g, 2)
                        pool.wait_ge(l_filled, late_use("oZ", g - 1) + 1)
                        met(pool)
                        for m in range(2):
                            for n in range(2):
                                pool.tensor_tensor(qbd[:, m, n, :, :],
                                                   qT[:, m, n * C:(n + 1) * C].unsqueeze(1).to_broadcast([128, 8, C]),
                                                   head_rows[:, :].unsqueeze(2).to_broadcast([128, 8, C]),
                                                   ALU.mult).then_inc(qbd_ready, 1)
                    if s == "OW":
                        at_pair(pool, ssq_ready, 1, g, 1)
                        at_pair(pool, an_ready, 1, g, 0)
                        met(pool)
                        pool.tensor_scalar(msq[:, :], ssq[:, :], 1.0 / S, EPS1, ALU.mult, ALU.add).then_inc(msq_ready, 1)
                        at_pair(pool, msq_ready, 1, g, 1)
                        met(pool)
                        pool.tensor_tensor(rs[:, :], msq[:, :], minus_half[:, :], ALU.pow).then_inc(rs_ready, 1)
                    if s in ("M1a", "M1b"):
                        i = "ab".index(s[2])
                        at_pair(pool, hu_ready, 2, g, i + 1)
                        at_pair(pool, th_ready, 2, g, i + 1 - 2)
                        met(pool)
                        pool.tensor_tensor(h2[:, i, :], hu[:, i, :], hu[:, i, :], ALU.mult).then_inc(h2_ready, 1)
                        at_pair(pool, h2_ready, 2, g, i + 1)
                        met(pool)
                        pool.tensor_scalar(h3[:, i, :], h2[:, i, :], GELU_C, 1.0, ALU.mult, ALU.add).then_inc(h3_ready, 1)
                        at_pair(pool, h3_ready, 2, g, i + 1)
                        met(pool)
                        pool.tensor_tensor(h2[:, i, :], h3[:, i, :], hu[:, i, :], ALU.mult).then_inc(inner_ready, 1)

            split_entry(0, 0)
            context_parts(0, 0)
            split_entry(0, 1)
            run(pool, "pool", step)

        @block.scalar
        def _(act):
            act.wait_ge(stat_pe, 2)
            act.wait_ge(memset_done, 6)
            nc.scalar.activation(std[:, :], t_bank[:, 64:64 + G], ACT.Sqrt, bias=zero_col[:, 0:1]).then_inc(std_ready, 1)

            def transposed(g, par):
                at_step(act, cT_done, 1, g, par, 1)
                at_step(act, x1T_ready, 1, g, par, -1)
                at_step(act, hc_ready, 1, g, par, -1)
                at_step(act, cf_ready, 2, g, par, -2)
                nc.scalar.activation(cx[par][:, :, :, :].rearrange("p a b c -> p (a b c)"), t_bank[:, 0:256],
                                     ACT.Copy).then_inc(cx_ready, 1)

            def query_high(g, par, i):
                at_step(act, q_filled, 10, g, par, i + 1)
                at_step(act, s_filled, 8, g, par, -8)
                q = qs[par][0:C, i * 1024:(i + 1) * 1024].rearrange("p (a e s) -> p a e s", a=2, e=2)
                for e in range(2):
                    nc.scalar.activation(q[:, :, e, :], q_bank[i][e * C:(e + 1) * C, :].rearrange("p (a s) -> p a s", a=2),
                                         ACT.Copy).then_inc(qhi_ready, 1)

            def neg_max(g, par):
                at_step(act, mT_done, 1, g, par, 1)
                at_step(act, row_loaded, 16, g, par, 0)
                nc.scalar.activation(nm[:, :], t_bank[0:2 * H0, 0:128], ACT.Copy, scale=-1.0).then_inc(nm_ready, 1)

            def step(g, par, names):
                ng, npar = other(par, g)
                for s in names:
                    if s == "cT":
                        transposed(ng, npar)
                    if s in ("qp0", "qp1"):
                        query_high(ng, npar, int(s[2]))
                    if s == "mT":
                        neg_max(ng, npar)
                    if s[:2] == "SB":
                        u = int(s[2])
                        at_step(act, s_filled, 8, g, par, u + 1)
                        at_step(act, plo_ready, 4, g, par, u // 2 - 3)
                        nc.scalar.activation(pT[:, u // 2, u % 2, :], s_bank[u % 2][:, :], ACT.Exp,
                                             scale=float(C) ** -0.5).then_inc(exp_done, 1)
                    if s[:2] == "HI":
                        p = int(s[2])
                        at_step(act, exp_done, 8, g, par, 2 * p + 2)
                        at_step(act, u_filled, 6, g, par, U_ORDER.index(f"U{p}") - 5)
                        nc.scalar.activation(ph[:, p, :, :], pT[:, p, :, :], ACT.Copy).then_inc(phi_ready, 1)
                    if s in ("O0", "O1"):
                        i = int(s[1])
                        at_step(act, u_filled, 6, g, par, 3 * i + 3)
                        if not (isinstance(g, int) and g == 0 and par == 0):
                            act.wait_ge(l_filled, late_use("oZ", g - 1) + 1 if par == 0 else late_use("eZ", g) + 1)
                        nc.scalar.activation(us[:, 2 * i:2 * i + 2, :].rearrange("p a s -> p (a s)"), u_bank[:, :],
                                             ACT.Copy).then_inc(us_ready, 1)
                    if s == "Q":
                        b = late_full(act, "Q", g)
                        at_pair(act, qbd_ready, 4, g, 0)
                        for m in range(2):
                            nc.scalar.activation(qT[:, m, :], b[:, m * 128:(m + 1) * 128], ACT.Identity,
                                                 bias=qb1[:, m:m + 1]).then_inc(qT_ready, 1)
                    if s == "K":
                        b = late_full(act, "K", g)
                        for m in range(2):
                            nc.scalar.activation(kT[:, m, :, :].rearrange("p n k -> p (n k)"), b[:, m * 256:(m + 1) * 256],
                                                 ACT.Identity, bias=kb1[:, m:m + 1]).then_inc(kT_ready, 1)
                    if s in ("S0", "S1", "S2", "S3"):
                        i = int(s[1])
                        at_pair(act, lsub_done, 4, g, i + 1)
                        nc.scalar.activation(px[:, i, :], sm[i % 2][:, :], ACT.Exp, scale=1.0 / D1).then_inc(lexp_done, 1)
                    if s in ("T0", "T1", "T2", "T3"):
                        i = int(s[1])
                        b = late_full(act, s, g)
                        nc.scalar.activation(pt1[:, i, :], b[:, :], ACT.Copy).then_inc(pt_ready, 1)
                    if s == "OT":
                        b = late_full(act, "OT", g)
                        nc.scalar.activation(oT[:, :, :].rearrange("p k c -> p (k c)"), b[:, 0:256], ACT.Copy).then_inc(oT_ready, 1)
                    if s == "AT":
                        b = late_full(act, "AT", g)
                        nc.scalar.activation(anT[:, :, :].rearrange("p k c -> p (k c)"), b[:, 0:256], ACT.Copy).then_inc(anT_ready, 1)
                    if s in ("TH0", "TH1"):
                        i = int(s[2])
                        at_pair(act, inner_ready, 2, g, i + 1)
                        nc.scalar.activation(th[:, i, :], h2[:, i, :], ACT.Tanh, scale=GELU_S).then_inc(th_ready, 1)

            transposed(0, 0)
            for i in range(2):
                query_high(0, 0, i)
            neg_max(0, 0)
            run(act, "act", step)

        @block.vector
        def _(dve):
            dve.memset(stat_ones[:, :], 0.0).then_inc(stat_dve, 1)
            dve.memset(cf[0][:, :, :, C:C + 1], 0.0).then_inc(stat_dve, 1)
            dve.memset(mask_row[:, :, :, :, :], 0.0).then_inc(stat_dve, 1)
            dve.memset(cf[1][:, :, :, C:C + 1], 0.0).then_inc(stat_dve, 1)
            for tile in (xh, cl[0], cl[1], qm[0], qm[1], w_lo):
                dve.memset(tile[C:128, :], 0.0).then_inc(stat_dve, 1)
            dve.wait_ge(stat_dve, 10)
            for r in range(2):
                dve.memset(stat_ones[r * C:(r + 1) * C, r * C:(r + 1) * C], 0.5 / C).then_inc(stat_dve, 1)
                dve.memset(cf[r][:, 0, :, C:C + 1], 1.0).then_inc(stat_dve, 1)
            dve.memset(ones_row[:, :], 1.0).then_inc(stat_dve, 1)
            dve.memset(xh[C:C + 1, :], 1.0).then_inc(stat_dve, 1)
            dve.memset(xh[96:97, :], 1.0).then_inc(stat_dve, 1)
            for i in range(2):
                dve.memset(xr[i][C:C + 1, :], 1.0).then_inc(memset_done, 1)
                dve.memset(cl[i][C:C + 1, :], 1.0).then_inc(memset_done, 1)
            dve.memset(zero_col[:, :], EPS0).then_inc(memset_done, 1)
            dve.wait_ge(stat_dve, 17)
            dve.memset(ssq[:, :], 0.0).then_inc(memset_done, 1)

            dve.wait_ge(prep_pe, 1)
            a_t, a_r = q_bank[0], q_bank[1]
            dve.tensor_copy(w_hi[0:C, :], a_t[0:C, :]).then_inc(prep_dve, 1)
            dve.tensor_copy(w_hi[C:128, :], a_t[0:C, :]).then_inc(prep_dve, 1)
            dve.tensor_copy(a_hi_row[:, :], a_r[0:1, :]).then_inc(prep_dve, 1)
            dve.wait_ge(prep_dve, 3)
            dve.tensor_tensor(w_lo[0:C, :], a_t[0:C, :], w_hi[0:C, :], ALU.subtract).then_inc(prep_dve, 1)
            dve.tensor_tensor(w_lo[96:97, :], a_r[0:1, :], a_hi_row[:, :], ALU.subtract).then_inc(prep_dve, 1)
            dve.tensor_copy(w_lo[C:C + 1, :], a_hi_row[:, :]).then_inc(prep_dve, 1)
            dve.wait_ge(prep_pe, 2)
            dve.tensor_copy(woT[:, :, :].rearrange("p h c -> p (h c)"), s_bank[0][0:C, :]).then_inc(prep_dve, 1)
            dve.wait_ge(prep_pe, 4)
            b_t = s_bank[1][0:C, :].rearrange("p (a e c) -> p a e c", a=4, e=2)
            for e in range(2):
                dve.tensor_copy(bd[e * C:(e + 1) * C, :, :], b_t[:, :, e, :]).then_inc(prep_dve, 1)
            dve.tensor_tensor(c0[:, :], u_bank[0:1, 0:C], bo[:, :], ALU.add).then_inc(prep_dve, 1)
            dve.wait_ge(const_ready, 7)
            dve.tensor_copy(x_const[0:C, :], ident[0:C, 0:C]).then_inc(prep_dve, 1)
            dve.wait_ge(prep_dve, 11)
            dve.tensor_copy(x_const[C:C + 1, :], c0[:, :]).then_inc(prep_dve, 1)

            for i in range(4):
                dve.wait_ge(xall_loaded[i], 16)
                with dve.Fori(8 * i, 8 * i + 8) as g:
                    dve.bn_stats(bn[:, bass.ds(g, 1), :, :].rearrange("p a b c -> p (a b c)"),
                                 x_all[:, bass.ds(g, 1), :].rearrange("p a s -> p (a s)")).then_inc(bn_done, 1)
            dve.wait_ge(stat_pe, 1)
            dve.wait_ge(bn_done, G)
            dve.tensor_tensor(dev[:, :, :], bn[:, :, :, 1], t_bank[:, 0:G].unsqueeze(2).to_broadcast([128, G, 2]),
                              ALU.subtract).then_inc(stat_dve, 1)
            dve.wait_ge(stat_dve, 18)
            dve.tensor_tensor(var_p[:, :, :], dev[:, :, :], dev[:, :, :], ALU.mult).then_inc(stat_dve, 1)
            dve.wait_ge(stat_dve, 19)
            dve.tensor_scalar(dev[:, :, :], bn[:, :, :, 2], 2.0 / S, None, ALU.mult).then_inc(stat_dve, 1)
            dve.wait_ge(stat_dve, 20)
            dve.tensor_tensor(var_p[:, :, :], var_p[:, :, :], dev[:, :, :], ALU.add).then_inc(stat_dve, 1)
            dve.wait_ge(std_ready, 1)
            dve.reciprocal(nscale[:, :], std[:, :]).then_inc(stat_dve, 1)
            dve.wait_ge(stat_dve, 22)
            dve.wait_ge(w0_loaded, 11 * 16)
            dve.tensor_scalar(nscale[:, :], nscale[:, :], gb[:, 0:1], None, ALU.mult).then_inc(stat_dve, 1)
            dve.wait_ge(stat_dve, 23)
            dve.tensor_tensor(nshift[:, :], t_bank[:, 0:G], nscale[:, :], ALU.mult).then_inc(stat_dve, 1)
            dve.wait_ge(stat_dve, 24)
            dve.tensor_scalar(nshift[:, :], nshift[:, :], -1.0, gb[:, 1:2], ALU.mult, ALU.add).then_inc(stat_dve, 1)
            dve.wait_ge(stat_dve, 25)
            for r in range(2):
                dve.tensor_copy(norm[:, :, r, 0], nscale[r * C:(r + 1) * C, :]).then_inc(stat_dve, 1)
                dve.tensor_copy(norm[:, :, r, 1], nshift[r * C:(r + 1) * C, :]).then_inc(stat_dve, 1)
            dve.wait_ge(stat_dve, 29)

            def normalise(g, par):
                dve.wait_ge(x_loaded[par], 16 * g + 16)
                at_step(dve, xpool, 3, g, par, 0)
                pair = g if isinstance(g, int) else bass.ds(g, 1)
                cols = [norm[:, g:g + 1, par, j] if isinstance(g, int) else norm[:, bass.ds(g, 1), par, j] for j in (0, 1)]
                dve.tensor_scalar(xn[:, :], xr[par][0:C, :], cols[0], cols[1], ALU.mult, ALU.add).then_inc(xn_ready, 1)

            def query_low(g, par, i):
                q = qs[par][:, i * 1024:(i + 1) * 1024].rearrange("p (a e s) -> p a e s", a=2, e=2)
                at_step(dve, qhi_ready, 4, g, par, 2 * i + 2)
                for e in range(2):
                    src = q_bank[i][e * C:(e + 1) * C, :].rearrange("p (a s) -> p a s", a=2)
                    dve.tensor_tensor(q[C:128, :, e, :], src, q[0:C, :, e, :], ALU.subtract).then_inc(qlo_ready, 1)

            def row_max(g, par, h):
                at_step(dve, q_filled, 10, g, par, 3 + h)
                at_step(dve, mT_done, 1, g, par, 0)
                dve.tensor_reduce(mx[:, 2 * h:2 * h + 2], q_bank[h % 2][:, :].rearrange("p (a k) -> p a k", a=2),
                                  AX.X, ALU.max).then_inc(max_done, 1)

            def step(g, par, names):
                ng, npar = other(par, g)
                for s in names:
                    if s in ("qp0", "qp1"):
                        query_low(ng, npar, int(s[2]))
                    if s[:2] == "SA":
                        row_max(ng, npar, int(s[2]))
                    if s == "NO" and not (isinstance(g, int) and g == G - 1):
                        normalise(g + 1, par)
                    if s[:2] == "LO":
                        p = int(s[2])
                        at_step(dve, phi_ready, 4, g, par, p + 1)
                        at_step(dve, u_filled, 6, g, par, U_ORDER.index(f"U{p}") - 5)
                        dve.tensor_tensor(pl[:, p, :, :], pT[:, p, :, :], ph[:, p, :, :], ALU.subtract).then_inc(plo_ready, 1)
                    if s in ("U0", "U1", "U2", "U3"):
                        p = int(s[1])
                        at_step(dve, u_filled, 6, g, par, U_ORDER.index(s) + 1)
                        at_step(dve, on_ready, 4, g, par, p - 3)
                        sums = u_bank[:, 0:4 * (C + 1)].rearrange("p (q e c) -> p q e c", q=2, e=2)
                        dve.reciprocal(rc[:, p, :, :], sums[:, :, :, C]).then_inc(rc_ready, 1)
                        at_step(dve, rc_ready, 4, g, par, p + 1)
                        dve.tensor_tensor(on[:, :, p, :, :], sums[:, :, :, 0:C],
                                          rc[:, p, :, :].unsqueeze(3).to_broadcast([128, 2, 2, C]), ALU.mult).then_inc(on_ready, 1)
                    if s == "Z":
                        b = late_full(dve, "eo"[par] + s, g)
                        if not (isinstance(g, int) and g == 0):
                            dve.wait_ge(l_filled, late_use("V", g) + 1)
                        dve.tensor_tensor(hT[:, :, 1 + par, :], b[:, 0:2 * C].rearrange("p (k c) -> p k c", k=2),
                                          cx[par][:, 1, :, :], ALU.add).then_inc(x1T_ready, 1)
                    if s == "X1":
                        b = late_full(dve, "X1", g)
                        at_pair(dve, fo_half, 1, g, 0)
                        dve.tensor_copy(x1[:, :], b[:, 0:S]).then_inc(x1_ready, 1)
                        at_pair(dve, pt_ready, 4, g, 0)
                        dve.tensor_scalar(mask_now[:, :, :].rearrange("p n k -> p (n k)"),
                                          mask_row[:, bass.ds(g - 1, 1), :, :, :].rearrange("p g n w c -> p (g n w c)"),
                                          1.0, None, ALU.mult).then_inc(mask_ready, 1)
                    if s == "V":
                        b = late_full(dve, "V", g)
                        bias = kvb[:, :].rearrange("p (h c w) -> p h c w", h=8, w=2)[:, :, :, 1]
                        for n in range(2):
                            dve.tensor_tensor(vx[:, n, :, 0:32], b[:, n * S:(n + 1) * S].rearrange("p (h c) -> p h c", h=8),
                                              bias, ALU.add).then_inc(v_ready, 1)
                    if s in ("S0", "S1", "S2", "S3"):
                        i = int(s[1])
                        b = late_full(dve, s, g)[:, :].rearrange("p (h k) -> p h k", h=4)
                        at_pair(dve, lsub_done, 4, g, i - 3)
                        dve.tensor_reduce(lmx[:, i, :], b, AX.X, ALU.max).then_inc(lmax_done, 1)
                        at_pair(dve, lmax_done, 4, g, i + 1)
                        at_pair(dve, lexp_done, 4, g, i - 1)
                        dve.tensor_tensor(sm[i % 2][:, :].rearrange("p (h k) -> p h k", h=4), b,
                                          lmx[:, i, :].unsqueeze(2).to_broadcast([128, 4, 128]), ALU.subtract).then_inc(lsub_done, 1)
                    if s in ("PV0", "PV1"):
                        n = int(s[2])
                        b = late_full(dve, s, g)[:, 0:264].rearrange("p (h c) -> p h c", h=8)
                        at_pair(dve, o1_ready, 4, g, 2 * n - 2)
                        dve.reciprocal(lrc[:, n, :], b[:, :, 32]).then_inc(lrc_ready, 1)
                        at_pair(dve, lrc_ready, 2, g, n + 1)
                        at_pair(dve, oT_ready, 1, g, 0)
                        for e in range(2):
                            rows = slice(e * C, (e + 1) * C)
                            dve.tensor_tensor(o1[n * C:(n + 1) * C, :].rearrange("p (h e d) -> p h e d", h=8, e=2)[:, :, e, :],
                                              b[rows, :, e * D1:(e + 1) * D1],
                                              lrc[rows, n, :].unsqueeze(2).to_broadcast([C, 8, D1]), ALU.mult).then_inc(o1_ready, 1)
                    if s == "OW":
                        b = late_full(dve, "OW", g)
                        at_pair(dve, an_ready, 1, g, 0)
                        dve.tensor_tensor(ao[:, :], b[:, 0:S], x1[:, :], ALU.add).then_inc(ao_raw, 1)
                        at_pair(dve, ao_raw, 1, g, 1)
                        dve.tensor_tensor(ao_b[:, :], ao[:, :], ob[:, :], ALU.add).then_inc(ao_ready, 1)
                        at_pair(dve, ao_ready, 1, g, 1)
                        at_pair(dve, msq_ready, 1, g, 0)
                        dve.tensor_tensor_reduce(sq[:, :], ao_b[:, :], ao_b[:, :], 1.0, 0.0, ALU.mult, ALU.add,
                                                 ssq[:, :]).then_inc(ssq_ready, 1)
                    if s == "RN":
                        at_pair(dve, rs_ready, 1, g, 1)
                        at_pair(dve, anT_ready, 1, g, 0)
                        dve.scalar_tensor_tensor(out=an[:, :], in0=ao_b[:, :], scalar=rs[:, 0:1], in1=pw[:, :],
                                                 op0=ALU.mult, op1=ALU.mult).then_inc(an_ready, 1)
                    if s in ("M1a", "M1b"):
                        i = "ab".index(s[2])
                        b = late_full(dve, s, g)[:, :].rearrange("p (m c) -> p m c", m=4)
                        at_pair(dve, gg_ready, 2, g, i + 1 - 2)
                        dve.tensor_tensor(hu[:, i, :].rearrange("p (m c) -> p m c", m=4), b,
                                          b1[:, 4 * i:4 * i + 4].unsqueeze(2).to_broadcast([128, 4, 128]), ALU.add).then_inc(hu_ready, 1)
                    if s in ("GG0", "GG1"):
                        i = int(s[2])
                        at_pair(dve, th_ready, 2, g, i + 1)
                        at_pair(dve, fo_half, 1, g, 0)
                        dve.scalar_tensor_tensor(out=gg[:, 4 * i:4 * i + 4, :].rearrange("p m c -> p (m c)"), in0=th[:, i, :],
                                                 scalar=1.0, in1=hu[:, i, :], op0=ALU.add, op1=ALU.mult).then_inc(gg_ready, 1)
                    if s == "M2":
                        b = late_full(dve, "M2", g)
                        at_pair(dve, fo_ready, 1, g, 0)
                        dve.scalar_tensor_tensor(out=fo[:, :], in0=b[:, 0:S], scalar=0.5, in1=x1[:, :],
                                                 op0=ALU.mult, op1=ALU.add).then_inc(fo_half, 1)
                        at_pair(dve, fo_half, 1, g, 1)
                        at_pair(dve, stored, 16, g, 0)
                        dve.tensor_tensor(fo_b[:, :], fo[:, :], b2[:, :], ALU.add).then_inc(fo_ready, 1)

            normalise(0, 0)
            for i in range(2):
                query_low(0, 0, i)
            normalise(0, 1)
            for h in range(H0):
                row_max(0, 0, h)
            dve.wait_ge(w1_loaded, 13 * 16)
            for k in range(2):
                pair = kvw[:, k, :].rearrange("p (c w) -> p c w", w=2)
                dve.tensor_copy(kw[:, k, :], pair[:, :, 0]).then_inc(l1_weights_ready, 1)
                dve.tensor_copy(vw[:, k, :], pair[:, :, 1]).then_inc(l1_weights_ready, 1)
            for n in range(2):
                dve.tensor_scalar(mask_row[:, :, n, n, :], mask_i.rearrange("p (g r) c -> p g r c", r=2)[:, :, n, :], 0.0, MASKED,
                                  ALU.is_equal, ALU.mult).then_inc(l1_weights_ready, 1)
            run(dve, "dve", step)

        @block.tensor
        def _(pe):
            mm = pe.matmul
            pe.wait_ge(w0_loaded, 11 * 16)
            for h in range(H0):
                mm(q_bank[0][0:C, h * C:(h + 1) * C], lhsT=wq[:, h, :], rhs=wk[:, h, :], start=True, stop=True)
                last = mm(q_bank[1][0:1, h * C:(h + 1) * C], lhsT=bq[:, h:h + 1], rhs=wk[:, h, :], start=True, stop=True)
            last.then_inc(prep_pe, 1)
            pe.wait_ge(const_ready, 7)
            for h in range(H0):
                last = pe.transpose(s_bank[0][0:C, h * C:(h + 1) * C], wo[:, h * C:(h + 1) * C], ident[0:C, 0:C])
            last.then_inc(prep_pe, 1)
            pe.wait_ge(prep_dve, 7)
            for h in range(H0):
                last = mm(s_bank[1][0:C, h * C:(h + 1) * C], lhsT=wv[:, h, :], rhs=woT[:, h, :], start=True, stop=True)
            last.then_inc(prep_pe, 1)
            for h in range(H0):
                last = mm(u_bank[0:1, 0:C], lhsT=bv[:, h:h + 1], rhs=woT[:, h, :], start=(h == 0), stop=(h == H0 - 1))
            last.then_inc(prep_pe, 1)
            pe.wait_ge(stat_dve, 17)
            pe.wait_ge(bn_done, G)
            for i in range(2):
                last = mm(t_bank[:, 0:G], lhsT=stat_ones[:, :], rhs=bn[:, :, i, 1], start=(i == 0), stop=(i == 1))
            last.then_inc(stat_pe, 1)
            pe.wait_ge(stat_dve, 21)
            for i in range(2):
                last = mm(t_bank[:, 64:64 + G], lhsT=stat_ones[:, :], rhs=var_p[:, :, i], start=(i == 0), stop=(i == 1))
            last.then_inc(stat_pe, 1)
            pe.wait_ge(prep_dve, 12)
            pe.wait_ge(stat_dve, 29)
            pe.wait_ge(memset_done, 6)

            def transposed(g, par):
                pe.wait_ge(c_loaded[par], 32 * g + 32)
                pe.wait_ge(x_loaded[par], 16 * g + 16)
                at_step(pe, nm_ready, 1, g, par, 0)
                for k in range(2):
                    mm(t_bank[:, 128 + k * C:128 + (k + 1) * C], lhsT=xr[par][:, k * 128:(k + 1) * 128],
                       rhs=x_const[:, :], start=True, stop=True)
                for k in range(2):
                    last = pe.transpose(t_bank[:, k * C:(k + 1) * C], c2[par][0:C, k * 128:(k + 1) * 128], ident[0:C, 0:C])
                last.then_inc(cT_done, 1)

            def queries(g, par, i):
                at_step(pe, xpool, 3, g, par, 3)
                at_step(pe, max_done, 8, g, par, -1 + i)
                for a in range(2):
                    out = q_bank[i][:, a * S:(a + 1) * S]
                    cols = slice((2 * i + a) * 128, (2 * i + a + 1) * 128)
                    mm(out, lhsT=w_hi[:, cols], rhs=xs[:, :], start=True, stop=False)
                    last = mm(out, lhsT=w_lo[:, cols], rhs=xh[:, :], start=False, stop=True)
                last.then_inc(q_filled, 1)

            def scores_by_query(g, par, h):
                at_step(pe, qlo_ready, 4, g, par, 2 if h < 4 else 4)
                if h < 2:
                    at_step(pe, qlo_ready, 4, g, par, 2 * h + 2)
                else:
                    at_step(pe, max_done, 8, g, par, h - 1)
                at_step(pe, cpool, 2, g, par, 1)
                for i in range(2):
                    last = mm(q_bank[h % 2][:, i * S:(i + 1) * S], lhsT=qs[par][:, h * S + i * 128:h * S + (i + 1) * 128],
                              rhs=ch[par][:, :], start=True, stop=True)
                last.then_inc(q_filled, 1)

            def max_rows(g, par):
                at_step(pe, max_done, 8, g, par, 8)
                at_step(pe, cx_ready, 1, g, par, 1)
                pe.transpose(t_bank[0:2 * H0, 0:128], mx[:, :], ident[:, :]).then_inc(mT_done, 1)

            def step(g, par, names):
                ng, npar = other(par, g)
                for s in names:
                    if s == "cT":
                        transposed(ng, npar)
                    if s in ("qp0", "qp1"):
                        queries(ng, npar, int(s[2]))
                    if s[:2] == "SA":
                        scores_by_query(ng, npar, int(s[2]))
                    if s == "mT":
                        max_rows(ng, npar)
                    if s[:2] == "SB":
                        u = int(s[2])
                        p, k = u // 2, u % 2
                        if u == 0:
                            at_step(pe, row_loaded, 16, g, par, 16)
                            pe.wait_ge(qm_loaded[par], 32 * g + 32)
                            at_step(pe, cpool, 2, g, par, 2)
                            at_step(pe, qlo_ready, 4, g, par, 4)
                        at_step(pe, exp_done, 8, g, par, u - 1)
                        cols, keys = slice(p * 512, (p + 1) * 512), slice(k * 128, (k + 1) * 128)
                        mm(s_bank[k][:, :], lhsT=ch[par][:, keys], rhs=qs[par][:, cols], start=True, stop=False)
                        mm(s_bank[k][:, :], lhsT=cl[par][:, keys], rhs=qm[par][:, cols], start=False, stop=True).then_inc(s_filled, 1)
                    if s in ("U0", "U1", "U2", "U3"):
                        p = int(s[1])
                        at_step(pe, plo_ready, 4, g, par, p + 1)
                        at_step(pe, cf_ready, 2, g, par, 2)
                        if p % 2:
                            at_step(pe, on_ready, 4, g, par, p)
                        else:
                            at_step(pe, us_ready, 2, g, par, p // 2)
                        for q in range(2):
                            for e in range(2):
                                out = u_bank[:, (2 * q + e) * (C + 1):(2 * q + e + 1) * (C + 1)]
                                cols = slice(e * S + q * 128, e * S + (q + 1) * 128)
                                for k in range(2):
                                    mm(out, lhsT=ph[:, p, k, cols], rhs=cf[par][:, 0, k, :], start=(k == 0), stop=False)
                                    mm(out, lhsT=ph[:, p, k, cols], rhs=cf[par][:, 1, k, :], start=False, stop=False)
                                    last = mm(out, lhsT=pl[:, p, k, cols], rhs=cf[par][:, 0, k, :], start=False, stop=(k == 1))
                        last.then_inc(u_filled, 1)
                    if s in ("O0", "O1"):
                        i = int(s[1])
                        at_step(pe, on_ready, 4, g, par, 2 * i + 2)
                        for p in range(2):
                            for q in range(2):
                                last = pe.transpose(u_bank[:, p * S + q * 128:p * S + (q + 1) * 128],
                                                    on[:, q, 2 * i + p, :, :].rearrange("p e c -> p (e c)"), ident[:, :])
                        last.then_inc(u_filled, 1)
                    if s == "Z":
                        at_step(pe, us_ready, 2, g, par, 2)
                        b = late_free(pe, "eo"[par] + s, g)
                        for q in range(2):
                            for p in range(4):
                                last = mm(b[:, q * C:(q + 1) * C], lhsT=us[:, p, q * 128:(q + 1) * 128], rhs=bd[:, p, :],
                                          start=(p == 0), stop=(p == 3))
                        last.then_inc(l_filled, 1)
                    if s == "X1":
                        if isinstance(g, int) and g == 1:
                            pe.wait_ge(l1_weights_ready, 6)
                        at_step(pe, x1T_ready, 1, g, 0, 0)
                        at_step(pe, hc_ready, 1, g, 0, 0)
                        b = late_free(pe, s, g)
                        for k in range(2):
                            last = pe.transpose(b[:, k * 128:(k + 1) * 128], hT[:, k, 1:3, :].rearrange("p n c -> p (n c)"), ident[:, :])
                        last.then_inc(l_filled, 1)
                    if s == "Q":
                        b = late_free(pe, s, g)
                        for m in range(2):
                            for k in range(2):
                                last = mm(b[:, m * 128:(m + 1) * 128], lhsT=qw[:, k, m * 128:(m + 1) * 128],
                                          rhs=hT[:, k, 1:3, :].rearrange("p n c -> p (n c)"), start=(k == 0), stop=(k == 1))
                        last.then_inc(l_filled, 1)
                    if s == "K":
                        b = late_free(pe, s, g)
                        for m in range(2):
                            for k in range(2):
                                last = mm(b[:, m * 256:(m + 1) * 256], lhsT=kw[:, k, m * 128:(m + 1) * 128],
                                          rhs=hT[:, k, :, :].rearrange("p n c -> p (n c)"), start=(k == 0), stop=(k == 1))
                        last.then_inc(l_filled, 1)
                    if s == "V":
                        b = late_free(pe, s, g)
                        for n in range(2):
                            for k in range(2):
                                last = mm(b[:, n * S:(n + 1) * S], lhsT=hT[:, k, 2 * n:2 * n + 2, :].rearrange("p w c -> p (w c)"),
                                          rhs=vw[:, k, :], start=(k == 0), stop=(k == 1))
                        last.then_inc(l_filled, 1)
                    if s in ("S0", "S1", "S2", "S3"):
                        n, m = int(s[1]) // 2, int(s[1]) % 2
                        at_pair(pe, kT_ready, 2, g, 2)
                        at_pair(pe, qbd_ready, 4, g, 2 * m + n + 1)
                        b = late_free(pe, s, g)
                        at_pair(pe, mask_ready, 1, g, 1)
                        mm(b[:, :].rearrange("p (h k) -> p h k", h=4), lhsT=ones_row[:, :],
                           rhs=mask_now[:, n:n + 1, :].to_broadcast([1, 4, 128]), start=True, stop=True)
                        for i in range(4):
                            last = mm(b[:, i * 128:(i + 1) * 128],
                                      lhsT=qbd[:, m, n, 2 * i:2 * i + 2, :].rearrange("p h c -> p (h c)"),
                                      rhs=kT[:, m, n, :], start=False, stop=True, skip_group_check=True)
                        last.then_inc(l_filled, 1)
                    if s in ("T0", "T1", "T2", "T3"):
                        i = int(s[1])
                        at_pair(pe, lexp_done, 4, g, i + 1)
                        b = late_free(pe, s, g)
                        for j in range(4):
                            last = pe.transpose(b[:, j * 128:(j + 1) * 128], px[:, i, j * 128:(j + 1) * 128], ident[:, :])
                        last.then_inc(l_filled, 1)
                    if s in ("PV0", "PV1"):
                        n = int(s[2])
                        at_pair(pe, pt_ready, 4, g, 2 * n + 2)
                        at_pair(pe, v_ready, 2, g, n + 1)
                        b = late_free(pe, s, g)
                        for i in range(8):
                            last = mm(b[:, i * 33:(i + 1) * 33], lhsT=pt1[:, 2 * n + i // 4, (i % 4) * 128:(i % 4 + 1) * 128],
                                      rhs=vx[:, n, i, :], start=True, stop=True)
                        last.then_inc(l_filled, 1)
                    if s == "OT":
                        at_pair(pe, o1_ready, 4, g, 4)
                        b = late_free(pe, s, g)
                        for k in range(2):
                            last = pe.transpose(b[:, k * 128:(k + 1) * 128], o1[:, k * 128:(k + 1) * 128], ident[:, :])
                        last.then_inc(l_filled, 1)
                    if s == "OW":
                        at_pair(pe, oT_ready, 1, g, 1)
                        b = late_free(pe, s, g)
                        for k in range(2):
                            last = mm(b[:, 0:S], lhsT=oT[:, k, :], rhs=ow[:, k, :], start=(k == 0), stop=(k == 1))
                        last.then_inc(l_filled, 1)
                    if s == "AT":
                        at_pair(pe, an_ready, 1, g, 1)
                        b = late_free(pe, s, g)
                        for k in range(2):
                            last = pe.transpose(b[:, k * 128:(k + 1) * 128], an[:, k * 128:(k + 1) * 128], ident[:, :])
                        last.then_inc(l_filled, 1)
                    if s in ("M1a", "M1b"):
                        i = "ab".index(s[2])
                        at_pair(pe, anT_ready, 1, g, 1)
                        b = late_free(pe, s, g)
                        for j in range(4):
                            m = 4 * i + j
                            for k in range(2):
                                last = mm(b[:, j * 128:(j + 1) * 128], lhsT=w1[:, k, m * 128:(m + 1) * 128], rhs=anT[:, k, :],
                                          start=(k == 0), stop=(k == 1))
                        last.then_inc(l_filled, 1)
                    if s == "M2":
                        b = late_free(pe, s, g)
                        for m in range(8):
                            at_pair(pe, gg_ready, 2, g, m // 4 + 1)
                            last = mm(b[:, 0:S], lhsT=gg[:, m, :], rhs=w2[:, m, :], start=(m == 0), stop=(m == 7))
                        last.then_inc(l_filled, 1)

            transposed(0, 0)
            for i in range(2):
                queries(0, 0, i)
            for h in range(H0):
                scores_by_query(0, 0, h)
            max_rows(0, 0)
            run(pe, "pe", step)


INPUTS = ["x", "ctx_2048", "mask_BxS2_ik0", "L0_xattn_gamma", "L0_xattn_beta", "L0_xattn_Wq", "L0_xattn_bq",
          "L0_xattn_Wkv", "L0_xattn_bkv", "L0_xattn_Wo", "L0_xattn_bo", "L1_xattn_q_w", "L1_xattn_q_b",
          "L1_xattn_kv_w", "L1_xattn_kv_b", "L1_xattn_out_w", "L1_xattn_out_b", "L1_xattn_postnorm_w",
          "L1_xattn_mlp_w1", "L1_xattn_mlp_b1", "L1_xattn_mlp_w2", "L1_xattn_mlp_b2"]


def kernel(**inputs):
    import numpy as np
    import concourse.bacc as bacc
    from concourse.bass_utils import run_bass_kernel_spmd

    nc = bacc.Bacc("TRN2", target_bir_lowering=False, num_devices=1)
    arrays, t = {}, {}
    for name in INPUTS:
        a = np.ascontiguousarray(inputs[name])
        arrays[f"in_{name}"] = a
        t[name] = nc.dram_tensor(f"in_{name}", a.shape, mybir.dt.from_np(a.dtype), kind="ExternalInput").ap()
    t["out"] = nc.dram_tensor("out_0", (N, C, S), F32, kind="ExternalOutput").ap()
    build(nc, t)
    r = run_bass_kernel_spmd(nc, [arrays], core_ids=[0])
    return r.results[0]["out_0"]
```

```python
from contextlib import ExitStack

import concourse.bass as bass
from concourse import mybir

F32 = mybir.dt.float32
F16 = mybir.dt.float16
BF16 = mybir.dt.bfloat16
I32 = mybir.dt.int32
ALU = mybir.AluOpType
ACT = mybir.ActivationFunctionType
AX = mybir.AxisListType

N, C, S = 64, 64, 256
H0 = 8
H1, D1 = 16, 16
FF = 4 * S
G = N // 2
MASKED = -1.0e30
GELU_C, GELU_S = 0.044715, 0.7978845608028654
EPS0, EPS1 = 1e-5, 1e-6

ORDER = {
    "pe": (
        "qp0 cT X1 SB0 qp1 SB1 Q SB2 SA0 K SB3 SA1 SB4 SA2 SB5 SA3 V SA4 SB6 SA5 U0 S0 SB7 U1 S1 S2 SA6 O0 S3 "
        "U2 T0 SA7 U3 mT T1 T2",
        "-O1 T3 qp0 PV0 SB0 qp1 SB1 PV1 -Z OT SB2 SA0 SB3 OW SB4 SB5 SA1 SA2 cT SB6 U0 AT SA3 SB7 U1 SA4 M1a "
        "O0 U2 SA5 U3 SA6 M1b O1 SA7 mT Z M2",
    ),
    "act": (
        "qp0 cT SB0 qp1 SB1 HI0 Q SB2 SB3 HI1 SB4 K SB5 SB6 HI2 SB7 S0 HI3 O0 S1 S2 T0 S3 mT T1 T2 O1",
        "qp0 T3 SB0 SB1 qp1 HI0 OT SB2 SB3 SB4 HI1 cT SB5 SB6 HI2 AT SB7 HI3 O0 SQ0 O1 SQ1 mT TH0 TH1",
    ),
    "dve": (
        "qp0 X1 qp1 SA0 SA1 SA2 SA3 LO0 V SA4 U0 SA5 S0 U1 NO S1 SA6 S2 S3 SA7",
        "-U2 -U3 PV0 PV1 qp0 -Z qp1 SA0 OW RN SA1 U0 SA2 SA3 AL U1 LO2 NO SA4 M1a U2 SA5 U3 SA6 M1b SA7 GG0 "
        "GG1 Z M2",
    ),
    "pool": (
        "-SPL Q LO1 cT LO2 LO3 SPL HC",
        "LO0 OW LO1 LO3 HC cT M1a M1b",
    ),
    "sp": (
        "LD qp0 qp1 mT",
        "LD qp0 qp1 mT M2",
    ),
}
FRONT = ("cT", "qp0", "qp1", "mT") + tuple(f"SA{h}" for h in range(H0))
BACK = ("O0", "O1", "Z", "NO", "SPL", "HC", "LD") + tuple(f"SB{u}" for u in range(8)) + tuple(
    f"{x}{p}" for x in ("U", "HI", "LO") for p in range(4))
U_ORDER = ("U0", "U1", "O0", "U2", "U3", "O1")


def slots(eng, g, par):
    for s in ORDER[eng][par].split():
        if g is None:
            wanted = True
        elif s in FRONT:
            wanted = not (g == G or (g == G - 1 and par))
        elif s in BACK:
            wanted = g < G
        elif s[0] == "-":
            wanted = (g, par) != (0, 0) and (g, par) != (G, 1)
        else:
            wanted = g > 0
        if wanted:
            yield s


LATE_STEP = ("cT", "mT", "Z")


def late_uses(g):
    uses = []
    for par in (0, 1):
        for s in slots("pe", g, par):
            if s in LATE_STEP:
                uses.append("eo"[par] + s)
            elif s == "-Z":
                uses.append("-oZ" if par == 0 else "eZ")
            elif s not in FRONT and s not in BACK and s[0] != "-":
                uses.append(s)
    return uses


def late_before(g):
    first, every = len(late_uses(0)), len(late_uses(None))
    if isinstance(g, int):
        return 2 + sum(len(late_uses(i)) for i in range(g))
    return 2 + first + every * (g - 1)


def late_place(name, g):
    at = g if isinstance(g, int) else 3
    uses, before = late_uses(at), late_uses(at - 1) if at else []
    if name not in uses:
        g, at = g + 1, at + 1
        uses, before, name = late_uses(at), uses, "-" + name
    i = uses.index(name)
    return g, i, uses, before, (late_before(at) + i) % 2


def build(nc, t):
    ctx = ExitStack()
    with ctx:
        def sb(name, shape, dt=F32):
            return ctx.enter_context(nc.sbuf_tensor(name, shape, dt))

        def sem(name):
            return ctx.enter_context(nc.semaphore(name))

        ctx.enter_context(nc.allow_non_contiguous_dma(reason="bias vectors, one element a partition, once"))

        q_bank = [ctx.enter_context(nc.psum_tensor(f"q_bank{i}", [128, 512], F32)) for i in range(2)]
        s_bank = [ctx.enter_context(nc.psum_tensor(f"s_bank{i}", [128, 512], F32)) for i in range(2)]
        u_bank = [ctx.enter_context(nc.psum_tensor(f"u_bank{i}", [128, 512], F32)) for i in range(2)]
        l_bank = [ctx.enter_context(nc.psum_tensor(f"l_bank{i}", [128, 512], F32)) for i in range(2)]

        ident = sb("ident", [128, 128])
        stat_ones = sb("stat_ones", [128, 128])
        head_rows = sb("head_rows", [128, 8])
        ones_row = sb("ones_row", [1, 128], BF16)
        minus_half = sb("minus_half", [128, 1])
        zero_col = sb("zero_col", [128, 1])
        wq = sb("wq", [C, H0, C])
        wk = sb("wk", [C, H0, C])
        wv = sb("wv", [C, H0, C])
        wo = sb("wo", [C, H0 * C])
        woT = sb("woT", [C, H0, C])
        bq = sb("bq", [C, H0])
        bv = sb("bv", [C, H0])
        bo = sb("bo", [1, C])
        gb = sb("gb", [128, 2])
        a_hi_row = sb("a_hi_row", [1, 512], F16)
        w_hi = sb("w_hi", [128, 512], F16)
        w_lo = sb("w_lo", [128, 512], F16)
        bd = sb("bd", [128, 4, C])
        x_const = sb("x_const", [C + 1, C])
        c0 = sb("c0", [1, C])
        qw = sb("qw", [128, 2, S])
        kvw = sb("kvw", [128, 2, 2 * S])
        kw = sb("kw", [128, 2, S])
        vw = sb("vw", [128, 2, S])
        ow = sb("ow", [128, 2, S])
        w1_hi = sb("w1_hi", [128, 2, FF], F16)
        w1_lo = sb("w1_lo", [128, 2, FF], F16)
        w2 = sb("w2", [128, 8, S])
        qb1 = sb("qb1", [128, 2])
        kb1 = sb("kb1", [128, 2])
        b1 = sb("b1", [128, 8])
        kvb = sb("kvb", [128, 2 * S])
        ob = sb("ob", [128, S])
        pw = sb("pw", [128, S])
        b2 = sb("b2", [128, S])
        mask_row = sb("mask_row", [1, G, 2, 2, C], BF16)

        x_all = sb("x_all", [128, G, S])
        bn = sb("bn", [128, G, 2, 3])
        dev = sb("dev", [128, G, 2])
        var_p = sb("var_p", [128, G, 2])
        std = sb("std", [128, G])
        nscale = sb("nscale", [128, G])
        nshift = sb("nshift", [128, G])
        norm = sb("norm", [C, G, 2, 2])

        xr = [sb(f"xr{i}", [C + 1, S]) for i in range(2)]
        c2 = [sb(f"c2{i}", [128, S]) for i in range(2)]
        xn = sb("xn", [C, S])
        xs = sb("xs", [128, S], F16)
        xh = sb("xh", [128, S], F16)
        ch = [sb(f"ch{i}", [128, S], F16) for i in range(2)]
        cl = [sb(f"cl{i}", [128, S], F16) for i in range(2)]
        cx = [sb(f"cx{i}", [128, 2, 2, C]) for i in range(2)]
        qs = [sb(f"qs{i}", [128, H0 * S], F16) for i in range(2)]
        qm = [sb(f"qm{i}", [128, H0 * S], F16) for i in range(2)]
        mx = sb("mx", [128, 2 * H0])
        nm = sb("nm", [2 * H0, 128], F16)
        pT = x_all[:, 0:G // 2, :].rearrange("p (h k a) s -> p h k (a s)", h=4, k=2)
        ph, pl = (x_all[:, i * G // 4:(i + 1) * G // 4, :].rearrange("p a s -> p (a s)").bitcast(F16)
                  .rearrange("p (h k s) -> p h k s", h=4, k=2) for i in (2, 3))
        cf = [sb(f"cf{i}", [128, 2, 2, C + 1], F16) for i in range(2)]
        rc = sb("rc", [128, 4, 2, 2])
        on = sb("on", [128, 2, 4, 2, C])
        us = sb("us", [128, 4, S])

        hT = sb("hT", [128, 2, 4, C])
        x1 = sb("x1", [128, S])
        qT = sb("qT", [128, 2, 128])
        qbd = sb("qbd", [128, 2, 2, 8, C])
        kT = sb("kT", [128, 2, 2, 128])
        vx = sb("vx", [128, 2, 8, 33])
        lmx = sb("lmx", [128, 4, 4])
        sm = [sb(f"sm{i}", [128, 512]) for i in range(2)]
        px = sb("px", [128, 4, 512])
        pt1 = sb("pt1", [128, 4, 512])
        w1 = px[:, :, :].rearrange("p a b -> p (a b)").rearrange("p (k n) -> p k n", k=2)
        lrc = sb("lrc", [128, 2, 8])
        o1 = sb("o1", [128, S])
        oT = sb("oT", [128, 2, 128])
        ao = sb("ao", [128, S])
        ao_b = sb("ao_b", [128, S])
        sq = sb("sq", [128, S])
        ssq = sb("ssq", [128, 1])
        msq = sb("msq", [128, 1])
        rs = sb("rs", [128, 1])
        an = sb("an", [128, S])
        an_hi = sb("an_hi", [128, 2, 128], F16)
        an_lo = sb("an_lo", [128, 2, 128], F16)
        gelu_tiles = sb("gelu_tiles", [128, 4, 2, 512])
        mask_now = sb("mask_now", [1, 2, 128], BF16)
        hu, h2, h3, th = (gelu_tiles[:, i, :, :] for i in range(4))
        mask_i = gelu_tiles[0:1, :, :, :].rearrange("p a b c -> p (a b c)").bitcast(I32)[:, 0:N * C].rearrange("p (n c) -> p n c", n=N)
        gg = sb("gg", [128, 8, 128])
        fo = sb("fo", [128, S])
        fo_b = sb("fo_b", [128, S])

        w0_loaded = sem("w0_loaded")
        w1_loaded = sem("w1_loaded")
        xall_loaded = [sem(f"xall_loaded{i}") for i in range(4)]
        const_ready = sem("const_ready")
        memset_done = sem("memset_done")
        prep_pe = sem("prep_pe")
        prep_dve = sem("prep_dve")
        prep_act = sem("prep_act")
        stat_dve = sem("stat_dve")
        bn_done = sem("bn_done")
        stat_pe = sem("stat_pe")
        std_ready = sem("std_ready")
        l1_weights_ready = sem("l1_weights_ready")
        x_loaded = [sem(f"x_loaded{i}") for i in range(2)]
        c_loaded = [sem(f"c_loaded{i}") for i in range(2)]
        xn_ready = sem("xn_ready")
        xpool = sem("xpool")
        cpool = sem("cpool")
        cx_ready = sem("cx_ready")
        q_filled = sem("q_filled")
        qhi_ready = sem("qhi_ready")
        qlo_ready = sem("qlo_ready")
        qm_loaded = [sem(f"qm_loaded{i}") for i in range(2)]
        max_done = sem("max_done")
        nm_ready = sem("nm_ready")
        row_loaded = sem("row_loaded")
        s_filled = sem("s_filled")
        exp_done = sem("exp_done")
        u_filled = sem("u_filled")
        phi_ready = sem("phi_ready")
        plo_ready = [sem(f"plo_ready{p}") for p in range(4)]
        cf_ready = sem("cf_ready")
        rc_ready = sem("rc_ready")
        on_ready = sem("on_ready")
        us_ready = sem("us_ready")
        l_filled = sem("l_filled")
        x1T_ready = sem("x1T_ready")
        hc_ready = sem("hc_ready")
        mask_ready = sem("mask_ready")
        x1_ready = sem("x1_ready")
        qT_ready = sem("qT_ready")
        qbd_ready = sem("qbd_ready")
        kT_ready = sem("kT_ready")
        v_ready = sem("v_ready")
        lmax_done = sem("lmax_done")
        lsub_done = sem("lsub_done")
        lexp_done = sem("lexp_done")
        pt_ready = sem("pt_ready")
        lrc_ready = sem("lrc_ready")
        o1_ready = sem("o1_ready")
        oT_ready = sem("oT_ready")
        ao_raw = sem("ao_raw")
        ao_ready = sem("ao_ready")
        ssq_ready = sem("ssq_ready")
        msq_ready = sem("msq_ready")
        rs_ready = sem("rs_ready")
        an_ready = sem("an_ready")
        an_hi_ready = sem("an_hi_ready")
        anT_ready = sem("anT_ready")
        w1_hi_ready = sem("w1_hi_ready")
        w1_lo_ready = sem("w1_lo_ready")
        hu_ready = sem("hu_ready")
        h2_ready = sem("h2_ready")
        h3_ready = sem("h3_ready")
        inner_ready = sem("inner_ready")
        th_ready = sem("th_ready")
        gg_ready = sem("gg_ready")
        fo_half = sem("fo_half")
        fo_ready = sem("fo_ready")
        stored = sem("stored")
        waits_met = [sem("waits_met_gpsimd"), sem("waits_met_sync")]

        def at_step(eng, s, per, g, par, j):
            v = 2 * per * g + (per * par + j)
            if not isinstance(g, int) or v > 0:
                eng.wait_ge(s, v)

        def at_pair(eng, s, per, g, j):
            v = per * g + (j - per)
            if not isinstance(g, int) or v > 0:
                eng.wait_ge(s, v)

        def met(eng):
            eng.sem_inc(waits_met[eng is nc.sync], 1)

        drained = {"X1": (x1_ready, 1, 0), "Q": (qT_ready, 2, 0), "K": (kT_ready, 2, 0),
                   "V": (v_ready, 2, 0), "PV0": (o1_ready, 4, -2), "PV1": (o1_ready, 4, 0),
                   "OT": (oT_ready, 1, 0), "OW": (ao_raw, 1, 0), "AT": (anT_ready, 1, 0),
                   "M1a": (hu_ready, 2, -1), "M1b": (hu_ready, 2, 0), "M2": (fo_half, 1, 0),
                   "eZ": (x1T_ready, 2, 1), "oZ": (x1T_ready, 2, 2), "-oZ": (x1T_ready, 2, 0),
                   "ecT": (cx_ready, 2, 2), "ocT": (cx_ready, 2, 3),
                   "emT": (nm_ready, 2, 2), "omT": (nm_ready, 2, 3)}
        for i in range(4):
            drained[f"S{i}"] = (lsub_done, 4, i - 3)
            drained[f"T{i}"] = (pt_ready, 4, i - 3)

        def late_free(eng, name, g):
            g, i, uses, before, bank = late_place(name, g)
            if i >= 2:
                s, per, count = drained[uses[i - 2]]
                eng.wait_ge(s, per * g + count)
            elif before:
                s, per, count = drained[before[i - 2]]
                eng.wait_ge(s, per * (g - 1) + count)
            else:
                eng.wait_ge((cx_ready, nm_ready)[i], 1)
            return l_bank[bank]

        def late_full(eng, name, g):
            g, i, _, _, bank = late_place(name, g)
            eng.wait_ge(l_filled, late_before(g) + i + 1)
            return l_bank[bank]

        def after_late(eng, name, g):
            g, i, _, _, _ = late_place(name, g)
            eng.wait_ge(l_filled, late_before(g) + i + 1)

        def other(par, g):
            return (g, 1) if par == 0 else (g + 1, 0)

        def before(par, g):
            return (g - 1, 1) if par == 0 else (g, 0)

        block = ctx.enter_context(nc.Block())

        def run(eng, name, step):
            for g in range(2):
                for par in (0, 1):
                    step(g, par, slots(name, g, par))
            with eng.Fori(2, G - 1) as g:
                for par in (0, 1):
                    step(g, par, slots(name, None, par))
            for g in (G - 1, G):
                for par in (0, 1):
                    step(g, par, slots(name, g, par))

        @block.sync
        def _(sp):
            sp.dma_start(wq[:, :, :], t["L0_xattn_Wq"].rearrange("(h o) c -> o h c", h=H0)).then_inc(w0_loaded, 16)
            kv = t["L0_xattn_Wkv"].rearrange("(w h o) d -> w o h d", w=2, h=H0)
            sp.dma_start(wk[:, :, :], kv[0]).then_inc(w0_loaded, 16)
            sp.dma_start(wv[:, :, :], kv[1]).then_inc(w0_loaded, 16)
            sp.dma_start(wo[:, :], t["L0_xattn_Wo"]).then_inc(w0_loaded, 16)
            sp.dma_start(bq[:, :], t["L0_xattn_bq"].rearrange("(h o) -> o h", h=H0)).then_inc(w0_loaded, 16)
            sp.dma_start(bv[:, :], t["L0_xattn_bkv"].rearrange("(w h o) -> w o h", w=2, h=H0)[1]).then_inc(w0_loaded, 16)
            sp.dma_start(bo[:, :], t["L0_xattn_bo"].rearrange("(a c) -> a c", a=1)).then_inc(w0_loaded, 16)
            for r in range(2):
                for j, name in enumerate(("gamma", "beta")):
                    sp.dma_start(gb[r * C:(r + 1) * C, j:j + 1],
                                 t[f"L0_xattn_{name}"].rearrange("(c a) -> c a", a=1)).then_inc(w0_loaded, 16)

            def load_entry(g, par):
                n = 2 * g + par
                sp.dma_start(xr[par][0:C, :], t["x"][bass.ds(n, 1)].rearrange("a c s -> (a c) s")).then_inc(x_loaded[par], 16)
                for r in range(2):
                    sp.dma_start(c2[par][r * C:(r + 1) * C, :],
                                 t["ctx_2048"][bass.ds(n, 1)].rearrange("a c s -> (a c) s")).then_inc(c_loaded[par], 16)

            x_v = t["x"].rearrange("(g r) c s -> (r c) g s", r=2)
            for i in range(4):
                sp.dma_start(x_all[:, 8 * i:8 * i + 8, :], x_v[:, 8 * i:8 * i + 8, :]).then_inc(xall_loaded[i], 16)
                if i == 0:
                    load_entry(0, 0)
                    load_entry(0, 1)
            for dst, name, k in ((qw, "q_w", 2), (kvw, "kv_w", 2), (ow, "out_w", 2), (w1, "mlp_w1", 2), (w2, "mlp_w2", 8)):
                sp.dma_start(dst[:, :, :], t[f"L1_xattn_{name}"].rearrange("(k p) n -> p k n", k=k)).then_inc(w1_loaded, 16)
            sp.dma_start(qb1[:, :], t["L1_xattn_q_b"].rearrange("(k p) -> p k", k=2)).then_inc(w1_loaded, 16)
            sp.dma_start(kb1[:, :], t["L1_xattn_kv_b"].rearrange("(k p w) -> w p k", k=2, w=2)[0]).then_inc(w1_loaded, 16)
            sp.dma_start(b1[:, :], t["L1_xattn_mlp_b1"].rearrange("(k p) -> p k", k=8)).then_inc(w1_loaded, 16)
            for dst, name in ((kvb, "kv_b"), (ob, "out_b"), (pw, "postnorm_w"), (b2, "mlp_b2")):
                sp.dma_start(dst[:, :], t[f"L1_xattn_{name}"].partition_broadcast(128)).then_inc(w1_loaded, 16)
            sp.dma_start(mask_i[:, :, :], t["mask_BxS2_ik0"].rearrange("(a n) s -> a n s", a=1)).then_inc(w1_loaded, 16)

            def row(g, par):
                at_step(sp, nm_ready, 1, g, par, 1)
                met(sp)
                at_step(sp, s_filled, 8, g, par, -8)
                met(sp)
                sp.dma_start(qm[par][C:C + 1, :], nm[:, :]).then_inc(row_loaded, 16)

            def query_copy(g, par, i):
                at_step(sp, qhi_ready, 4, g, par, 2 * i + 2)
                met(sp)
                at_step(sp, s_filled, 8, g, par, -8)
                met(sp)
                cols = slice(i * 1024, (i + 1) * 1024)
                sp.dma_start(qm[par][0:C, cols], qs[par][0:C, cols]).then_inc(qm_loaded[par], 16)

            for i in range(2):
                query_copy(0, 0, i)
            sp.wait_ge(memset_done, 6)
            row(0, 0)

            def step(g, par, names):
                for s in names:
                    if s[0] == "-":
                        step(*before(par, g), [s[1:]])
                    if s == "LD" and not (isinstance(g, int) and g == G - 1):
                        at_step(sp, cx_ready, 1, g, par, 1)
                        met(sp)
                        at_step(sp, xn_ready, 1, g, par, 1)
                        met(sp)
                        at_step(sp, cpool, 2, g, par, 2)
                        met(sp)
                        load_entry(g + 1, par)
                    if s in ("qp0", "qp1"):
                        query_copy(*other(par, g), int(s[2]))
                    if s == "mT":
                        row(*other(par, g))
                    if s == "M2":
                        at_pair(sp, fo_ready, 1, g, 1)
                        met(sp)
                        dst = t["out"][bass.ds(2 * g - 2, 2)].rearrange("n c s -> (n c) s")
                        sp.dma_start(dst, fo_b[:, :]).then_inc(stored, 16)

            run(sp, "sp", step)
            sp.wait_ge(stored, 16 * G)

        @block.gpsimd
        def _(pool):
            pool.memset(ident[:, :], 0.0).then_inc(const_ready, 1)
            pool.memset(head_rows[:, :], 1.0).then_inc(const_ready, 1)
            pool.wait_ge(const_ready, 2)
            pool.affine_select(out=ident[:, :], in_=ident[:, :], compare_op=ALU.not_equal, fill=1.0, base=0,
                               pattern=[[-1, 128]], channel_multiplier=1).then_inc(const_ready, 1)
            pool.affine_select(out=head_rows[:, :], in_=head_rows[:, :], compare_op=ALU.is_ge, fill=0.0, base=0,
                               pattern=[[-D1, 8]], channel_multiplier=1).then_inc(const_ready, 1)
            pool.wait_ge(const_ready, 4)
            pool.affine_select(out=head_rows[:, :], in_=head_rows[:, :], compare_op=ALU.is_ge, fill=0.0, base=D1 - 1,
                               pattern=[[D1, 8]], channel_multiplier=-1).then_inc(const_ready, 1)
            pool.memset(minus_half[:, :], -0.5).then_inc(const_ready, 1)
            pool.memset(vx[:, :, :, 32:33], 1.0).then_inc(const_ready, 1)
            pool.wait_ge(const_ready, 7)
            pool.wait_ge(memset_done, 6)

            def split_entry(g, par):
                at_step(pool, xn_ready, 1, g, par, 1)
                at_step(pool, q_filled, 10, g, par, -8)
                met(pool)
                pool.tensor_scalar(xs[0:C, :], xn[:, :], 1.0, None, ALU.mult).then_inc(xpool, 1)
                pool.tensor_scalar(xh[0:C, :], xn[:, :], 1.0, None, ALU.mult).then_inc(xpool, 1)
                at_step(pool, xpool, 3, g, par, 2)
                met(pool)
                pool.tensor_tensor(xs[C:128, :], xn[:, :], xs[0:C, :], ALU.subtract).then_inc(xpool, 1)
                at_step(pool, xpool, 3, g, par, 3)
                pool.wait_ge(c_loaded[par], 32 * g + 32)
                at_step(pool, s_filled, 8, g, par, -8)
                met(pool)
                pool.tensor_scalar(ch[par][:, :], c2[par][:, :], 1.0, None, ALU.mult).then_inc(cpool, 1)
                at_step(pool, cpool, 2, g, par, 1)
                met(pool)
                pool.tensor_tensor(cl[par][0:C, :], c2[par][0:C, :], ch[par][0:C, :], ALU.subtract).then_inc(cpool, 1)

            def context_parts(g, par):
                at_step(pool, cx_ready, 1, g, par, 1)
                at_step(pool, u_filled, 6, g, par, -7)
                met(pool)
                pool.tensor_scalar(cf[par][:, 0, :, 0:C], cx[par][:, 0, :, :], 1.0, None, ALU.mult).then_inc(cf_ready, 1)
                at_step(pool, cf_ready, 2, g, par, 1)
                pool.tensor_tensor(cf[par][:, 1, :, 0:C], cx[par][:, 0, :, :], cf[par][:, 0, :, 0:C],
                                   ALU.subtract).then_inc(cf_ready, 1)

            def step(g, par, names):
                for s in names:
                    if s[0] == "-":
                        step(*before(par, g), [s[1:]])
                    if s == "cT":
                        context_parts(*other(par, g))
                    if s == "SPL" and not (isinstance(g, int) and g == G - 1):
                        split_entry(g + 1, par)
                    if s == "HC":
                        if par == 0 and not (isinstance(g, int) and g == 0):
                            after_late(pool, "V", g)
                            met(pool)
                        pool.tensor_copy(hT[:, :, 3 * par, :], cx[par][:, 0, :, :]).then_inc(hc_ready, 1)
                        if isinstance(g, int) and g == 0 and par == 0:
                            pool.wait_ge(w1_hi_ready, 1)
                            pool.tensor_tensor(w1_lo[:, :, :], w1, w1_hi[:, :, :], ALU.subtract).then_inc(w1_lo_ready, 1)
                    if s[:2] == "LO":
                        p = int(s[2])
                        at_step(pool, phi_ready, 4, g, par, p + 1)
                        met(pool)
                        pool.tensor_tensor(pl[:, p, :, :], pT[:, p, :, :], ph[:, p, :, :], ALU.subtract).then_inc(plo_ready[p], 1)
                    if s == "Q":
                        at_pair(pool, qT_ready, 2, g, 2)
                        met(pool)
                        for m in range(2):
                            for n in range(2):
                                pool.tensor_tensor(qbd[:, m, n, :, :],
                                                   qT[:, m, n * C:(n + 1) * C].unsqueeze(1).to_broadcast([128, 8, C]),
                                                   head_rows[:, :].unsqueeze(2).to_broadcast([128, 8, C]),
                                                   ALU.mult).then_inc(qbd_ready, 1)
                    if s == "OW":
                        at_pair(pool, ssq_ready, 1, g, 1)
                        met(pool)
                        pool.tensor_scalar(msq[:, :], ssq[:, :], 1.0 / S, EPS1, ALU.mult, ALU.add).then_inc(msq_ready, 1)
                        at_pair(pool, msq_ready, 1, g, 1)
                        met(pool)
                        pool.tensor_tensor(rs[:, :], msq[:, :], minus_half[:, :], ALU.pow).then_inc(rs_ready, 1)
                    if s in ("M1a", "M1b"):
                        i = "ab".index(s[2])
                        at_pair(pool, h2_ready, 2, g, i + 1)
                        met(pool)
                        pool.tensor_scalar(h3[:, i, :], h2[:, i, :], GELU_C, 1.0, ALU.mult, ALU.add).then_inc(h3_ready, 1)
                        at_pair(pool, h3_ready, 2, g, i + 1)
                        met(pool)
                        pool.tensor_tensor(h2[:, i, :], h3[:, i, :], hu[:, i, :], ALU.mult).then_inc(inner_ready, 1)

            split_entry(0, 0)
            context_parts(0, 0)
            split_entry(0, 1)
            run(pool, "pool", step)

        @block.scalar
        def _(act):
            act.wait_ge(prep_pe, 1)
            for r in range(2):
                nc.scalar.activation(w_hi[r * C:(r + 1) * C, :], q_bank[0][0:C, :], ACT.Copy).then_inc(prep_act, 1)
            act.wait_ge(prep_pe, 2)
            nc.scalar.activation(woT[:, :, :].rearrange("p h c -> p (h c)"), s_bank[0][0:C, :], ACT.Copy).then_inc(prep_act, 1)
            act.wait_ge(prep_pe, 3)
            b_t = s_bank[1][0:C, :].rearrange("p (a e c) -> p a e c", a=4, e=2)
            for e in range(2):
                nc.scalar.activation(bd[e * C:(e + 1) * C, :, :], b_t[:, :, e, :], ACT.Copy).then_inc(prep_act, 1)
            act.wait_ge(stat_pe, 2)
            act.wait_ge(memset_done, 6)
            nc.scalar.activation(std[:, :], l_bank[0][:, 64:64 + G], ACT.Sqrt, bias=zero_col[:, 0:1]).then_inc(std_ready, 1)

            def transposed(g, par, bank):
                at_step(act, x1T_ready, 1, g, par, -1)
                at_step(act, hc_ready, 1, g, par, -1)
                at_step(act, cf_ready, 2, g, par, -2)
                nc.scalar.activation(cx[par][:, :, :, :].rearrange("p a b c -> p (a b c)"), bank[:, 0:256],
                                     ACT.Copy).then_inc(cx_ready, 1)

            def query_high(g, par, i):
                at_step(act, q_filled, 10, g, par, i + 1)
                if i == 0:
                    at_step(act, s_filled, 8, g, par, -8)
                q = qs[par][0:C, i * 1024:(i + 1) * 1024].rearrange("p (a e s) -> p a e s", a=2, e=2)
                for e in range(2):
                    nc.scalar.activation(q[:, :, e, :], q_bank[i][e * C:(e + 1) * C, :].rearrange("p (a s) -> p a s", a=2),
                                         ACT.Copy).then_inc(qhi_ready, 1)

            def neg_max(g, par, bank):
                at_step(act, row_loaded, 16, g, par, 0)
                nc.scalar.activation(nm[:, :], bank[0:2 * H0, 0:128], ACT.Copy, scale=-1.0).then_inc(nm_ready, 1)

            def step(g, par, names):
                ng, npar = other(par, g)
                for s in names:
                    if s[0] == "-":
                        step(*before(par, g), [s[1:]])
                    if s == "cT":
                        transposed(ng, npar, late_full(act, "eo"[par] + s, g))
                    if s in ("qp0", "qp1"):
                        query_high(ng, npar, int(s[2]))
                    if s == "mT":
                        neg_max(ng, npar, late_full(act, "eo"[par] + s, g))
                    if s[:2] == "SB":
                        u = int(s[2])
                        at_step(act, s_filled, 8, g, par, u + 1)
                        if u % 2 == 0:
                            at_step(act, plo_ready[u // 2], 1, g, par, 0)
                        nc.scalar.activation(pT[:, u // 2, u % 2, :], s_bank[u % 2][:, :], ACT.Exp,
                                             scale=float(C) ** -0.5).then_inc(exp_done, 1)
                    if s[:2] == "HI":
                        p = int(s[2])
                        at_step(act, exp_done, 8, g, par, 2 * p + 2)
                        if p % 2 == 0:
                            at_step(act, u_filled, 6, g, par, U_ORDER.index(f"U{p + 1}") - 5)
                        nc.scalar.activation(ph[:, p, :, :], pT[:, p, :, :], ACT.Copy).then_inc(phi_ready, 1)
                    if s in ("O0", "O1"):
                        i = int(s[1])
                        at_step(act, u_filled, 6, g, par, 3 * i + 3)
                        if i == 0 and not (isinstance(g, int) and g == 0 and par == 0):
                            after_late(act, *(("oZ", g - 1) if par == 0 else ("eZ", g)))
                        nc.scalar.activation(us[:, 2 * i:2 * i + 2, :].rearrange("p a s -> p (a s)"), u_bank[U_ORDER.index(s) % 2][:, :],
                                             ACT.Copy).then_inc(us_ready, 1)
                    if s == "Q":
                        b = late_full(act, "Q", g)
                        at_pair(act, qbd_ready, 4, g, 0)
                        for m in range(2):
                            nc.scalar.activation(qT[:, m, :], b[:, m * 128:(m + 1) * 128], ACT.Identity,
                                                 bias=qb1[:, m:m + 1]).then_inc(qT_ready, 1)
                    if s == "K":
                        b = late_full(act, "K", g)
                        for m in range(2):
                            nc.scalar.activation(kT[:, m, :, :].rearrange("p n k -> p (n k)"), b[:, m * 256:(m + 1) * 256],
                                                 ACT.Identity, bias=kb1[:, m:m + 1]).then_inc(kT_ready, 1)
                    if s in ("S0", "S1", "S2", "S3"):
                        i = int(s[1])
                        at_pair(act, lsub_done, 4, g, i + 1)
                        nc.scalar.activation(px[:, i, :], sm[i % 2][:, :], ACT.Exp, scale=1.0 / D1).then_inc(lexp_done, 1)
                    if s in ("T0", "T1", "T2", "T3"):
                        i = int(s[1])
                        b = late_full(act, s, g)
                        nc.scalar.activation(pt1[:, i, :], b[:, :], ACT.Copy).then_inc(pt_ready, 1)
                    if s == "OT":
                        b = late_full(act, "OT", g)
                        nc.scalar.activation(oT[:, :, :].rearrange("p k c -> p (k c)"), b[:, 0:256], ACT.Copy).then_inc(oT_ready, 1)
                    if s == "AT":
                        b = late_full(act, "AT", g)
                        nc.scalar.activation(an_hi[:, :, :].rearrange("p k c -> p (k c)"), b[:, 0:256],
                                             ACT.Copy).then_inc(an_hi_ready, 1)
                    if s in ("SQ0", "SQ1"):
                        i = int(s[2])
                        at_pair(act, hu_ready, 2, g, i + 1)
                        nc.scalar.activation(h2[:, i, :], hu[:, i, :], ACT.Square).then_inc(h2_ready, 1)
                    if s in ("TH0", "TH1"):
                        i = int(s[2])
                        at_pair(act, inner_ready, 2, g, i + 1)
                        nc.scalar.activation(th[:, i, :], h2[:, i, :], ACT.Tanh, scale=GELU_S).then_inc(th_ready, 1)

            act.wait_ge(l_filled, 1)
            transposed(0, 0, l_bank[0])
            for i in range(2):
                query_high(0, 0, i)
            act.wait_ge(w1_loaded, 13 * 16)
            nc.scalar.activation(w1_hi[:, :, :], w1, ACT.Copy).then_inc(w1_hi_ready, 1)
            act.wait_ge(l_filled, 2)
            neg_max(0, 0, l_bank[1])
            run(act, "act", step)

        @block.vector
        def _(dve):
            dve.memset(stat_ones[:, :], 0.0).then_inc(stat_dve, 1)
            dve.memset(cf[0][:, :, :, C:C + 1], 0.0).then_inc(stat_dve, 1)
            dve.memset(mask_row[:, :, :, :, :], 0.0).then_inc(stat_dve, 1)
            dve.memset(cf[1][:, :, :, C:C + 1], 0.0).then_inc(stat_dve, 1)
            for tile in (xh, cl[0], cl[1], qm[0], qm[1], w_lo):
                dve.memset(tile[C:128, :], 0.0).then_inc(stat_dve, 1)
            dve.wait_ge(stat_dve, 10)
            for r in range(2):
                dve.memset(stat_ones[r * C:(r + 1) * C, r * C:(r + 1) * C], 0.5 / C).then_inc(stat_dve, 1)
                dve.memset(cf[r][:, 0, :, C:C + 1], 1.0).then_inc(stat_dve, 1)
            dve.memset(ones_row[:, :], 1.0).then_inc(stat_dve, 1)
            dve.memset(xh[C:C + 1, :], 1.0).then_inc(stat_dve, 1)
            dve.memset(xh[96:97, :], 1.0).then_inc(stat_dve, 1)
            for i in range(2):
                dve.memset(xr[i][C:C + 1, :], 1.0).then_inc(memset_done, 1)
                dve.memset(cl[i][C:C + 1, :], 1.0).then_inc(memset_done, 1)
            dve.memset(zero_col[:, :], EPS0).then_inc(memset_done, 1)
            dve.wait_ge(stat_dve, 17)
            dve.memset(ssq[:, :], 0.0).then_inc(memset_done, 1)

            def entry_stats(i):
                dve.wait_ge(xall_loaded[i], 16)
                with dve.Fori(G // 16 * i, G // 16 * (i + 1)) as quad:
                    for j in range(4):
                        g = 4 * quad + j
                        dve.bn_stats(bn[:, bass.ds(g, 1), :, :].rearrange("p a b c -> p (a b c)"),
                                     x_all[:, bass.ds(g, 1), :].rearrange("p a s -> p (a s)")).then_inc(bn_done, 1)

            for i in (0, 1):
                entry_stats(i)
            dve.wait_ge(prep_pe, 1)
            a_t, a_r = q_bank[0], q_bank[1]
            dve.tensor_copy(a_hi_row[:, :], a_r[0:1, :]).then_inc(prep_dve, 1)
            dve.wait_ge(prep_dve, 1)
            dve.tensor_tensor(w_lo[96:97, :], a_r[0:1, :], a_hi_row[:, :], ALU.subtract).then_inc(prep_dve, 1)
            dve.tensor_copy(w_lo[C:C + 1, :], a_hi_row[:, :]).then_inc(prep_dve, 1)
            dve.wait_ge(prep_act, 2)
            dve.tensor_tensor(w_lo[0:C, :], a_t[0:C, :], w_hi[0:C, :], ALU.subtract).then_inc(prep_dve, 1)
            for i in (2, 3):
                entry_stats(i)
            dve.wait_ge(const_ready, 7)
            dve.tensor_copy(x_const[0:C, :], ident[0:C, 0:C]).then_inc(prep_dve, 1)
            dve.wait_ge(prep_pe, 4)
            dve.tensor_tensor(c0[:, :], u_bank[0][0:1, 0:C], bo[:, :], ALU.add).then_inc(prep_dve, 1)
            dve.wait_ge(prep_dve, 6)
            dve.tensor_copy(x_const[C:C + 1, :], c0[:, :]).then_inc(prep_dve, 1)
            dve.wait_ge(stat_pe, 1)
            dve.wait_ge(bn_done, G)
            dve.tensor_tensor(dev[:, :, :], bn[:, :, :, 1], l_bank[0][:, 0:G].unsqueeze(2).to_broadcast([128, G, 2]),
                              ALU.subtract).then_inc(stat_dve, 1)
            dve.wait_ge(stat_dve, 18)
            dve.tensor_tensor(var_p[:, :, :], dev[:, :, :], dev[:, :, :], ALU.mult).then_inc(stat_dve, 1)
            dve.wait_ge(stat_dve, 19)
            dve.tensor_scalar(dev[:, :, :], bn[:, :, :, 2], 2.0 / S, None, ALU.mult).then_inc(stat_dve, 1)
            dve.wait_ge(stat_dve, 20)
            dve.tensor_tensor(var_p[:, :, :], var_p[:, :, :], dev[:, :, :], ALU.add).then_inc(stat_dve, 1)
            dve.wait_ge(std_ready, 1)
            dve.reciprocal(nscale[:, :], std[:, :]).then_inc(stat_dve, 1)
            dve.wait_ge(stat_dve, 22)
            dve.wait_ge(w0_loaded, 11 * 16)
            dve.tensor_scalar(nscale[:, :], nscale[:, :], gb[:, 0:1], None, ALU.mult).then_inc(stat_dve, 1)
            dve.wait_ge(stat_dve, 23)
            dve.tensor_tensor(nshift[:, :], l_bank[0][:, 0:G], nscale[:, :], ALU.mult).then_inc(stat_dve, 1)
            dve.wait_ge(stat_dve, 24)
            dve.tensor_scalar(nshift[:, :], nshift[:, :], -1.0, gb[:, 1:2], ALU.mult, ALU.add).then_inc(stat_dve, 1)
            dve.wait_ge(stat_dve, 25)
            for r in range(2):
                dve.tensor_copy(norm[:, :, r, 0], nscale[r * C:(r + 1) * C, :]).then_inc(stat_dve, 1)
                dve.tensor_copy(norm[:, :, r, 1], nshift[r * C:(r + 1) * C, :]).then_inc(stat_dve, 1)
            dve.wait_ge(stat_dve, 29)

            def normalise(g, par):
                dve.wait_ge(x_loaded[par], 16 * g + 16)
                at_step(dve, xpool, 3, g, par, 0)
                pair = g if isinstance(g, int) else bass.ds(g, 1)
                cols = [norm[:, g:g + 1, par, j] if isinstance(g, int) else norm[:, bass.ds(g, 1), par, j] for j in (0, 1)]
                dve.tensor_scalar(xn[:, :], xr[par][0:C, :], cols[0], cols[1], ALU.mult, ALU.add).then_inc(xn_ready, 1)

            def query_low(g, par, i):
                q = qs[par][:, i * 1024:(i + 1) * 1024].rearrange("p (a e s) -> p a e s", a=2, e=2)
                at_step(dve, qhi_ready, 4, g, par, 2 * i + 2)
                for e in range(2):
                    src = q_bank[i][e * C:(e + 1) * C, :].rearrange("p (a s) -> p a s", a=2)
                    dve.tensor_tensor(q[C:128, :, e, :], src, q[0:C, :, e, :], ALU.subtract).then_inc(qlo_ready, 1)

            def row_max(g, par, h):
                at_step(dve, q_filled, 10, g, par, 3 + h)
                if h == 0:
                    at_step(dve, nm_ready, 1, g, par, 0)
                dve.tensor_reduce(mx[:, 2 * h:2 * h + 2], q_bank[h % 2][:, :].rearrange("p (a k) -> p a k", a=2),
                                  AX.X, ALU.max).then_inc(max_done, 1)

            def step(g, par, names):
                ng, npar = other(par, g)
                for s in names:
                    if s[0] == "-":
                        step(*before(par, g), [s[1:]])
                    if s in ("qp0", "qp1"):
                        query_low(ng, npar, int(s[2]))
                    if s[:2] == "SA":
                        row_max(ng, npar, int(s[2]))
                    if s == "NO" and not (isinstance(g, int) and g == G - 1):
                        normalise(g + 1, par)
                    if s[:2] == "LO":
                        p = int(s[2])
                        at_step(dve, phi_ready, 4, g, par, p + 1)
                        dve.tensor_tensor(pl[:, p, :, :], pT[:, p, :, :], ph[:, p, :, :], ALU.subtract).then_inc(plo_ready[p], 1)
                    if s in ("U0", "U1", "U2", "U3"):
                        p = int(s[1])
                        at_step(dve, u_filled, 6, g, par, U_ORDER.index(s) + 1)
                        sums = u_bank[U_ORDER.index(s) % 2][:, 0:4 * (C + 1)].rearrange("p (q e c) -> p q e c", q=2, e=2)
                        dve.reciprocal(rc[:, p, :, :], sums[:, :, :, C]).then_inc(rc_ready, 1)
                        at_step(dve, rc_ready, 4, g, par, p + 1)
                        dve.tensor_tensor(on[:, :, p, :, :], sums[:, :, :, 0:C],
                                          rc[:, p, :, :].unsqueeze(3).to_broadcast([128, 2, 2, C]), ALU.mult).then_inc(on_ready, 1)
                    if s == "Z":
                        b = late_full(dve, "eo"[par] + s, g)
                        if par == 0 and not (isinstance(g, int) and g == 0):
                            after_late(dve, "V", g)
                        dve.tensor_tensor(hT[:, :, 1 + par, :], b[:, 0:2 * C].rearrange("p (k c) -> p k c", k=2),
                                          cx[par][:, 1, :, :], ALU.add).then_inc(x1T_ready, 1)
                    if s == "X1":
                        b = late_full(dve, "X1", g)
                        at_pair(dve, fo_half, 1, g, 0)
                        dve.tensor_copy(x1[:, :], b[:, 0:S]).then_inc(x1_ready, 1)
                        dve.tensor_scalar(mask_now[:, :, :].rearrange("p n k -> p (n k)"),
                                          mask_row[:, bass.ds(g - 1, 1), :, :, :].rearrange("p g n w c -> p (g n w c)"),
                                          1.0, None, ALU.mult).then_inc(mask_ready, 1)
                    if s == "V":
                        b = late_full(dve, "V", g)
                        bias = kvb[:, :].rearrange("p (h c w) -> p h c w", h=8, w=2)[:, :, :, 1]
                        for n in range(2):
                            dve.tensor_tensor(vx[:, n, :, 0:32], b[:, n * S:(n + 1) * S].rearrange("p (h c) -> p h c", h=8),
                                              bias, ALU.add).then_inc(v_ready, 1)
                    if s in ("S0", "S1", "S2", "S3"):
                        i = int(s[1])
                        b = late_full(dve, s, g)[:, :].rearrange("p (h k) -> p h k", h=4)
                        dve.tensor_reduce(lmx[:, i, :], b, AX.X, ALU.max).then_inc(lmax_done, 1)
                        at_pair(dve, lmax_done, 4, g, i + 1)
                        at_pair(dve, lexp_done, 4, g, i - 1)
                        dve.tensor_tensor(sm[i % 2][:, :].rearrange("p (h k) -> p h k", h=4), b,
                                          lmx[:, i, :].unsqueeze(2).to_broadcast([128, 4, 128]), ALU.subtract).then_inc(lsub_done, 1)
                    if s in ("PV0", "PV1"):
                        n = int(s[2])
                        b = late_full(dve, s, g)[:, 0:264].rearrange("p (h c) -> p h c", h=8)
                        dve.reciprocal(lrc[:, n, :], b[:, :, 32]).then_inc(lrc_ready, 1)
                        at_pair(dve, lrc_ready, 2, g, n + 1)
                        for e in range(2):
                            rows = slice(e * C, (e + 1) * C)
                            dve.tensor_tensor(o1[n * C:(n + 1) * C, :].rearrange("p (h e d) -> p h e d", h=8, e=2)[:, :, e, :],
                                              b[rows, :, e * D1:(e + 1) * D1],
                                              lrc[rows, n, :].unsqueeze(2).to_broadcast([C, 8, D1]), ALU.mult).then_inc(o1_ready, 1)
                    if s == "OW":
                        b = late_full(dve, "OW", g)
                        dve.tensor_tensor(ao[:, :], b[:, 0:S], x1[:, :], ALU.add).then_inc(ao_raw, 1)
                        at_pair(dve, ao_raw, 1, g, 1)
                        dve.tensor_tensor(ao_b[:, :], ao[:, :], ob[:, :], ALU.add).then_inc(ao_ready, 1)
                        at_pair(dve, ao_ready, 1, g, 1)
                        dve.tensor_tensor_reduce(sq[:, :], ao_b[:, :], ao_b[:, :], 1.0, 0.0, ALU.mult, ALU.add,
                                                 ssq[:, :]).then_inc(ssq_ready, 1)
                    if s == "AL":
                        b = late_full(dve, "AT", g)
                        at_pair(dve, an_hi_ready, 1, g, 1)
                        dve.tensor_tensor(an_lo[:, :, :].rearrange("p k c -> p (k c)"), b[:, 0:256],
                                          an_hi[:, :, :].rearrange("p k c -> p (k c)"), ALU.subtract).then_inc(anT_ready, 1)
                    if s == "RN":
                        at_pair(dve, rs_ready, 1, g, 1)
                        dve.scalar_tensor_tensor(out=an[:, :], in0=ao_b[:, :], scalar=rs[:, 0:1], in1=pw[:, :],
                                                 op0=ALU.mult, op1=ALU.mult).then_inc(an_ready, 1)
                    if s in ("M1a", "M1b"):
                        i = "ab".index(s[2])
                        b = late_full(dve, s, g)[:, :].rearrange("p (m c) -> p m c", m=4)
                        dve.tensor_tensor(hu[:, i, :].rearrange("p (m c) -> p m c", m=4), b,
                                          b1[:, 4 * i:4 * i + 4].unsqueeze(2).to_broadcast([128, 4, 128]), ALU.add).then_inc(hu_ready, 1)
                    if s in ("GG0", "GG1"):
                        i = int(s[2])
                        at_pair(dve, th_ready, 2, g, i + 1)
                        dve.scalar_tensor_tensor(out=gg[:, 4 * i:4 * i + 4, :].rearrange("p m c -> p (m c)"), in0=th[:, i, :],
                                                 scalar=1.0, in1=hu[:, i, :], op0=ALU.add, op1=ALU.mult).then_inc(gg_ready, 1)
                    if s == "M2":
                        b = late_full(dve, "M2", g)
                        at_pair(dve, stored, 16, g, 0)
                        dve.scalar_tensor_tensor(out=fo[:, :], in0=b[:, 0:S], scalar=0.5, in1=x1[:, :],
                                                 op0=ALU.mult, op1=ALU.add).then_inc(fo_half, 1)
                        at_pair(dve, fo_half, 1, g, 1)
                        dve.tensor_tensor(fo_b[:, :], fo[:, :], b2[:, :], ALU.add).then_inc(fo_ready, 1)

            normalise(0, 0)
            for i in range(2):
                query_low(0, 0, i)
            normalise(0, 1)
            for h in range(H0):
                row_max(0, 0, h)
            dve.wait_ge(w1_loaded, 13 * 16)
            for k in range(2):
                pair = kvw[:, k, :].rearrange("p (c w) -> p c w", w=2)
                dve.tensor_copy(kw[:, k, :], pair[:, :, 0]).then_inc(l1_weights_ready, 1)
                dve.tensor_copy(vw[:, k, :], pair[:, :, 1]).then_inc(l1_weights_ready, 1)
            for n in range(2):
                dve.tensor_scalar(mask_row[:, :, n, n, :], mask_i.rearrange("p (g r) c -> p g r c", r=2)[:, :, n, :], 0.0, MASKED,
                                  ALU.is_equal, ALU.mult).then_inc(l1_weights_ready, 1)
            run(dve, "dve", step)

        @block.tensor
        def _(pe):
            mm = pe.matmul
            pe.wait_ge(w0_loaded, 11 * 16)
            for h in range(H0):
                mm(q_bank[0][0:C, h * C:(h + 1) * C], lhsT=wq[:, h, :], rhs=wk[:, h, :], start=True, stop=True)
                last = mm(q_bank[1][0:1, h * C:(h + 1) * C], lhsT=bq[:, h:h + 1], rhs=wk[:, h, :], start=True, stop=True)
            last.then_inc(prep_pe, 1)
            pe.wait_ge(const_ready, 7)
            for h in range(H0):
                last = pe.transpose(s_bank[0][0:C, h * C:(h + 1) * C], wo[:, h * C:(h + 1) * C], ident[0:C, 0:C])
            last.then_inc(prep_pe, 1)
            pe.wait_ge(prep_act, 3)
            for h in range(H0):
                last = mm(s_bank[1][0:C, h * C:(h + 1) * C], lhsT=wv[:, h, :], rhs=woT[:, h, :], start=True, stop=True)
            last.then_inc(prep_pe, 1)
            for h in range(H0):
                last = mm(u_bank[0][0:1, 0:C], lhsT=bv[:, h:h + 1], rhs=woT[:, h, :], start=(h == 0), stop=(h == H0 - 1))
            last.then_inc(prep_pe, 1)
            pe.wait_ge(stat_dve, 17)
            pe.wait_ge(bn_done, G)
            for i in range(2):
                last = mm(l_bank[0][:, 0:G], lhsT=stat_ones[:, :], rhs=bn[:, :, i, 1], start=(i == 0), stop=(i == 1))
            last.then_inc(stat_pe, 1)
            pe.wait_ge(stat_dve, 21)
            for i in range(2):
                last = mm(l_bank[0][:, 64:64 + G], lhsT=stat_ones[:, :], rhs=var_p[:, :, i], start=(i == 0), stop=(i == 1))
            last.then_inc(stat_pe, 1)
            pe.wait_ge(prep_dve, 7)
            pe.wait_ge(prep_act, 5)
            pe.wait_ge(stat_dve, 29)
            pe.wait_ge(memset_done, 6)

            def transposed(g, par, bank):
                pe.wait_ge(c_loaded[par], 32 * g + 32)
                pe.wait_ge(x_loaded[par], 16 * g + 16)
                for k in range(2):
                    mm(bank[:, 128 + k * C:128 + (k + 1) * C], lhsT=xr[par][:, k * 128:(k + 1) * 128],
                       rhs=x_const[:, :], start=True, stop=True)
                for k in range(2):
                    last = pe.transpose(bank[:, k * C:(k + 1) * C], c2[par][0:C, k * 128:(k + 1) * 128], ident[0:C, 0:C])
                last.then_inc(l_filled, 1)

            def queries(g, par, i):
                if i == 0:
                    at_step(pe, xpool, 3, g, par, 3)
                at_step(pe, max_done, 8, g, par, -1 + i)
                for a in range(2):
                    out = q_bank[i][:, a * S:(a + 1) * S]
                    cols = slice((2 * i + a) * 128, (2 * i + a + 1) * 128)
                    mm(out, lhsT=w_hi[:, cols], rhs=xs[:, :], start=True, stop=False)
                    last = mm(out, lhsT=w_lo[:, cols], rhs=xh[:, :], start=False, stop=True)
                last.then_inc(q_filled, 1)

            def scores_by_query(g, par, h):
                if h < 2:
                    at_step(pe, qlo_ready, 4, g, par, 2 * h + 2)
                else:
                    at_step(pe, max_done, 8, g, par, h - 1)
                if h == 0:
                    at_step(pe, cpool, 2, g, par, 1)
                for i in range(2):
                    last = mm(q_bank[h % 2][:, i * S:(i + 1) * S], lhsT=qs[par][:, h * S + i * 128:h * S + (i + 1) * 128],
                              rhs=ch[par][:, :], start=True, stop=True)
                last.then_inc(q_filled, 1)

            def max_rows(g, par, bank):
                at_step(pe, max_done, 8, g, par, 8)
                pe.transpose(bank[0:2 * H0, 0:128], mx[:, :], ident[:, :]).then_inc(l_filled, 1)

            def step(g, par, names):
                ng, npar = other(par, g)
                for s in names:
                    if s[0] == "-":
                        step(*before(par, g), [s[1:]])
                    if s == "cT":
                        transposed(ng, npar, late_free(pe, "eo"[par] + s, g))
                    if s in ("qp0", "qp1"):
                        queries(ng, npar, int(s[2]))
                    if s[:2] == "SA":
                        scores_by_query(ng, npar, int(s[2]))
                    if s == "mT":
                        max_rows(ng, npar, late_free(pe, "eo"[par] + s, g))
                    if s[:2] == "SB":
                        u = int(s[2])
                        p, k = u // 2, u % 2
                        if u == 0:
                            at_step(pe, row_loaded, 16, g, par, 16)
                            pe.wait_ge(qm_loaded[par], 32 * g + 32)
                            at_step(pe, cpool, 2, g, par, 2)
                            at_step(pe, qlo_ready, 4, g, par, 4)
                        at_step(pe, exp_done, 8, g, par, u - 1)
                        cols, keys = slice(p * 512, (p + 1) * 512), slice(k * 128, (k + 1) * 128)
                        mm(s_bank[k][:, :], lhsT=ch[par][:, keys], rhs=qs[par][:, cols], start=True, stop=False)
                        mm(s_bank[k][:, :], lhsT=cl[par][:, keys], rhs=qm[par][:, cols], start=False, stop=True).then_inc(s_filled, 1)
                    if s in ("U0", "U1", "U2", "U3"):
                        p = int(s[1])
                        at_step(pe, plo_ready[p], 1, g, par, 1)
                        if p == 0:
                            at_step(pe, cf_ready, 2, g, par, 2)
                        bank = u_bank[U_ORDER.index(s) % 2]
                        if p == 1 or p == 3:
                            at_step(pe, us_ready, 2, g, par, p // 2)
                        for q in range(2):
                            for e in range(2):
                                out = bank[:, (2 * q + e) * (C + 1):(2 * q + e + 1) * (C + 1)]
                                cols = slice(e * S + q * 128, e * S + (q + 1) * 128)
                                for k in range(2):
                                    mm(out, lhsT=ph[:, p, k, cols], rhs=cf[par][:, 0, k, :], start=(k == 0), stop=False)
                                    mm(out, lhsT=ph[:, p, k, cols], rhs=cf[par][:, 1, k, :], start=False, stop=False)
                                    last = mm(out, lhsT=pl[:, p, k, cols], rhs=cf[par][:, 0, k, :], start=False, stop=(k == 1))
                        last.then_inc(u_filled, 1)
                    if s in ("O0", "O1"):
                        i = int(s[1])
                        at_step(pe, on_ready, 4, g, par, 2 * i + 2)
                        bank = u_bank[U_ORDER.index(s) % 2]
                        for p in range(2):
                            for q in range(2):
                                last = pe.transpose(bank[:, p * S + q * 128:p * S + (q + 1) * 128],
                                                    on[:, q, 2 * i + p, :, :].rearrange("p e c -> p (e c)"), ident[:, :])
                        last.then_inc(u_filled, 1)
                    if s == "Z":
                        at_step(pe, us_ready, 2, g, par, 2)
                        b = late_free(pe, "eo"[par] + s, g)
                        for q in range(2):
                            for p in range(4):
                                last = mm(b[:, q * C:(q + 1) * C], lhsT=us[:, p, q * 128:(q + 1) * 128], rhs=bd[:, p, :],
                                          start=(p == 0), stop=(p == 3))
                        last.then_inc(l_filled, 1)
                    if s == "X1":
                        if isinstance(g, int) and g == 1:
                            pe.wait_ge(l1_weights_ready, 6)
                            pe.wait_ge(w1_lo_ready, 1)
                        at_step(pe, x1T_ready, 1, g, 0, 0)
                        at_step(pe, hc_ready, 1, g, 0, 0)
                        b = late_free(pe, s, g)
                        for k in range(2):
                            last = pe.transpose(b[:, k * 128:(k + 1) * 128], hT[:, k, 1:3, :].rearrange("p n c -> p (n c)"), ident[:, :])
                        last.then_inc(l_filled, 1)
                    if s == "Q":
                        b = late_free(pe, s, g)
                        for m in range(2):
                            for k in range(2):
                                last = mm(b[:, m * 128:(m + 1) * 128], lhsT=qw[:, k, m * 128:(m + 1) * 128],
                                          rhs=hT[:, k, 1:3, :].rearrange("p n c -> p (n c)"), start=(k == 0), stop=(k == 1))
                        last.then_inc(l_filled, 1)
                    if s == "K":
                        b = late_free(pe, s, g)
                        for m in range(2):
                            for k in range(2):
                                last = mm(b[:, m * 256:(m + 1) * 256], lhsT=kw[:, k, m * 128:(m + 1) * 128],
                                          rhs=hT[:, k, :, :].rearrange("p n c -> p (n c)"), start=(k == 0), stop=(k == 1))
                        last.then_inc(l_filled, 1)
                    if s == "V":
                        b = late_free(pe, s, g)
                        for n in range(2):
                            for k in range(2):
                                last = mm(b[:, n * S:(n + 1) * S], lhsT=hT[:, k, 2 * n:2 * n + 2, :].rearrange("p w c -> p (w c)"),
                                          rhs=vw[:, k, :], start=(k == 0), stop=(k == 1))
                        last.then_inc(l_filled, 1)
                    if s in ("S0", "S1", "S2", "S3"):
                        n, m = int(s[1]) // 2, int(s[1]) % 2
                        if s == "S0":
                            at_pair(pe, kT_ready, 2, g, 2)
                        at_pair(pe, qbd_ready, 4, g, 2 * m + n + 1)
                        b = late_free(pe, s, g)
                        if s == "S0":
                            at_pair(pe, mask_ready, 1, g, 1)
                        mm(b[:, :].rearrange("p (h k) -> p h k", h=4), lhsT=ones_row[:, :],
                           rhs=mask_now[:, n:n + 1, :].to_broadcast([1, 4, 128]), start=True, stop=True)
                        for i in range(4):
                            last = mm(b[:, i * 128:(i + 1) * 128],
                                      lhsT=qbd[:, m, n, 2 * i:2 * i + 2, :].rearrange("p h c -> p (h c)"),
                                      rhs=kT[:, m, n, :], start=False, stop=True, skip_group_check=True)
                        last.then_inc(l_filled, 1)
                    if s in ("T0", "T1", "T2", "T3"):
                        i = int(s[1])
                        at_pair(pe, lexp_done, 4, g, i + 1)
                        b = late_free(pe, s, g)
                        for j in range(4):
                            last = pe.transpose(b[:, j * 128:(j + 1) * 128], px[:, i, j * 128:(j + 1) * 128], ident[:, :])
                        last.then_inc(l_filled, 1)
                    if s in ("PV0", "PV1"):
                        n = int(s[2])
                        at_pair(pe, pt_ready, 4, g, 2 * n + 2)
                        at_pair(pe, v_ready, 2, g, n + 1)
                        b = late_free(pe, s, g)
                        for i in range(8):
                            last = mm(b[:, i * 33:(i + 1) * 33], lhsT=pt1[:, 2 * n + i // 4, (i % 4) * 128:(i % 4 + 1) * 128],
                                      rhs=vx[:, n, i, :], start=True, stop=True)
                        last.then_inc(l_filled, 1)
                    if s == "OT":
                        at_pair(pe, o1_ready, 4, g, 4)
                        b = late_free(pe, s, g)
                        for k in range(2):
                            last = pe.transpose(b[:, k * 128:(k + 1) * 128], o1[:, k * 128:(k + 1) * 128], ident[:, :])
                        last.then_inc(l_filled, 1)
                    if s == "OW":
                        at_pair(pe, oT_ready, 1, g, 1)
                        b = late_free(pe, s, g)
                        for k in range(2):
                            last = mm(b[:, 0:S], lhsT=oT[:, k, :], rhs=ow[:, k, :], start=(k == 0), stop=(k == 1))
                        last.then_inc(l_filled, 1)
                    if s == "AT":
                        at_pair(pe, an_ready, 1, g, 1)
                        b = late_free(pe, s, g)
                        for k in range(2):
                            last = pe.transpose(b[:, k * 128:(k + 1) * 128], an[:, k * 128:(k + 1) * 128], ident[:, :])
                        last.then_inc(l_filled, 1)
                    if s in ("M1a", "M1b"):
                        i = "ab".index(s[2])
                        if i == 0:
                            at_pair(pe, anT_ready, 1, g, 1)
                        b = late_free(pe, s, g)
                        for j in range(4):
                            m = 4 * i + j
                            for part, (w, x) in enumerate(((w1_hi, an_hi), (w1_hi, an_lo), (w1_lo, an_hi))):
                                for k in range(2):
                                    last = mm(b[:, j * 128:(j + 1) * 128], lhsT=w[:, k, m * 128:(m + 1) * 128], rhs=x[:, k, :],
                                              start=(part == 0 and k == 0), stop=(part == 2 and k == 1))
                        last.then_inc(l_filled, 1)
                    if s == "M2":
                        b = late_free(pe, s, g)
                        for m in range(8):
                            at_pair(pe, gg_ready, 2, g, m // 4 + 1)
                            last = mm(b[:, 0:S], lhsT=gg[:, m, :], rhs=w2[:, m, :], start=(m == 0), stop=(m == 7))
                        last.then_inc(l_filled, 1)

            transposed(0, 0, l_bank[0])
            for i in range(2):
                queries(0, 0, i)
            for h in range(H0):
                scores_by_query(0, 0, h)
            max_rows(0, 0, l_bank[1])
            run(pe, "pe", step)


INPUTS = ["x", "ctx_2048", "mask_BxS2_ik0", "L0_xattn_gamma", "L0_xattn_beta", "L0_xattn_Wq", "L0_xattn_bq",
          "L0_xattn_Wkv", "L0_xattn_bkv", "L0_xattn_Wo", "L0_xattn_bo", "L1_xattn_q_w", "L1_xattn_q_b",
          "L1_xattn_kv_w", "L1_xattn_kv_b", "L1_xattn_out_w", "L1_xattn_out_b", "L1_xattn_postnorm_w",
          "L1_xattn_mlp_w1", "L1_xattn_mlp_b1", "L1_xattn_mlp_w2", "L1_xattn_mlp_b2"]


def kernel(**inputs):
    import numpy as np
    import concourse.bacc as bacc
    from concourse.bass_utils import run_bass_kernel_spmd

    nc = bacc.Bacc("TRN2", target_bir_lowering=False, num_devices=1)
    arrays, t = {}, {}
    for name in INPUTS:
        a = np.ascontiguousarray(inputs[name])
        arrays[f"in_{name}"] = a
        t[name] = nc.dram_tensor(f"in_{name}", a.shape, mybir.dt.from_np(a.dtype), kind="ExternalInput").ap()
    t["out"] = nc.dram_tensor("out_0", (N, C, S), F32, kind="ExternalOutput").ap()
    build(nc, t)
    r = run_bass_kernel_spmd(nc, [arrays], core_ids=[0])
    return r.results[0]["out_0"]
```
